# Optimizing a Trainium2 kernel written in Bass

```python
import numpy as np
import jax
import jax.numpy as jnp

def _softmax(x, axis=-1):
    return jax.nn.softmax(x, axis=axis)

def _gelu(x):
    return jax.nn.gelu(x, approximate=True)

def _silu(x):
    return jax.nn.silu(x)

def _sigmoid(x):
    return jax.nn.sigmoid(x)

def _layernorm(x, axis=-1, eps=1e-05):
    m = jnp.mean(x, axis=axis, keepdims=True)
    v = jnp.var(x, axis=axis, keepdims=True)
    return (x - m) / jnp.sqrt(v + eps)

def _scatter_add(tgt, idx, src, axis=0):
    return tgt.at[idx].add(src)

def _segment_sum(src, seg, n):
    return jax.ops.segment_sum(src, seg, n)
kernel_name = 'mk_vit_tower_d1_tok_img768_r4_dde462'

def setup_inputs(seed: int=0):
    np.random.seed(seed)
    _w = jnp.asarray

    def _rec_inputs():
        import jax
        import jax.numpy as jnp
        _rk = jax.random.key(seed)
        x = -0.00040386 + 0.999972 * jax.random.normal(jax.random.fold_in(_rk, 1), (2, 3, 64, 64), jnp.float32)
        return x
    x = _rec_inputs()

    def _L0_tok_setup():
        import jax, jax.numpy as jnp
        import numpy as np
        PATCH = 4
        SHIFT = PATCH // 2
        EMBED = 192
        PATCH_DIM = 3 * 3 * PATCH * PATCH
        key = jax.random.key(seed)
        k1, k2 = jax.random.split(key)
        x = jax.random.normal(k1, (64, 3, 64, 64), dtype=jnp.float32)
        ln_gamma = jnp.ones((PATCH_DIM,), dtype=jnp.float32)
        ln_beta = jnp.zeros((PATCH_DIM,), dtype=jnp.float32)
        W = jax.random.normal(k2, (PATCH_DIM, EMBED), dtype=jnp.float32) * 0.02
        b = jnp.zeros((EMBED,), dtype=jnp.float32)
        return {'x': x, 'ln_gamma': ln_gamma, 'ln_beta': ln_beta, 'W': W, 'b': b}
    _L0_tok_all = _L0_tok_setup()
    _L0_tok_in = {k: v for k, v in _L0_tok_all.items() if k in ('ln_gamma', 'ln_beta', 'W', 'b')}
    del _L0_tok_all

    def _L0_attn_setup():
        import jax, jax.numpy as jnp
        import numpy as np
        B, S, D, H = (8, 256, 192, 12)
        HS = D // H
        key = jax.random.key(seed)
        k1, k2, k3 = jax.random.split(key, 3)
        x = jax.random.normal(k1, (B, S, D), dtype=jnp.float32)
        W_attn = jax.random.normal(k2, (D, 3 * H * HS), dtype=jnp.float32) * 0.02
        b_attn = jnp.zeros((3 * H * HS,), dtype=jnp.float32)
        W_proj = jax.random.normal(k3, (H * HS, D), dtype=jnp.float32) * 0.02
        b_proj = jnp.zeros((D,), dtype=jnp.float32)
        return {'x': x, 'W_attn': W_attn, 'b_attn': b_attn, 'W_proj': W_proj, 'b_proj': b_proj}
    _L0_attn_all = _L0_attn_setup()
    _L0_attn_in = {k: v for k, v in _L0_attn_all.items() if k in ('W_attn', 'b_attn', 'W_proj', 'b_proj')}
    del _L0_attn_all

    def _L0_ffn_setup():
        import jax, jax.numpy as jnp
        import numpy as np
        DIM = 192
        HIDDEN = 192
        NUM_EXPERTS = 4
        B, S = (16, 512)
        key = jax.random.key(seed)
        ks = jax.random.split(key, 7)
        sd = 1.0 / np.sqrt(DIM)
        sh = 1.0 / np.sqrt(HIDDEN)
        return {'x': jax.random.normal(ks[0], (B, S, DIM), dtype=jnp.float32), 'router_w': jax.random.uniform(ks[1], (DIM, NUM_EXPERTS), jnp.float32, -sd, sd), 'router_b': jax.random.uniform(ks[2], (NUM_EXPERTS,), jnp.float32, -sd, sd), 'w1': jax.random.uniform(ks[3], (NUM_EXPERTS, DIM, HIDDEN), jnp.float32, -sd, sd), 'b1': jax.random.uniform(ks[4], (NUM_EXPERTS, HIDDEN), jnp.float32, -sd, sd), 'w2': jax.random.uniform(ks[5], (NUM_EXPERTS, HIDDEN, DIM), jnp.float32, -sd, sd), 'b2': jax.random.uniform(ks[6], (NUM_EXPERTS, DIM), jnp.float32, -sd, sd)}
    _L0_ffn_all = _L0_ffn_setup()
    _L0_ffn_in = {k: v for k, v in _L0_ffn_all.items() if k in ('router_w', 'router_b', 'w1', 'b1', 'w2', 'b2')}
    del _L0_ffn_all
    return {'x': x, 'L0_tok_ln_gamma': _L0_tok_in['ln_gamma'], 'L0_tok_ln_beta': _L0_tok_in['ln_beta'], 'L0_tok_W': _L0_tok_in['W'], 'L0_tok_b': _L0_tok_in['b'], 'L0_attn_W_attn': _L0_attn_in['W_attn'], 'L0_attn_b_attn': _L0_attn_in['b_attn'], 'L0_attn_W_proj': _L0_attn_in['W_proj'], 'L0_attn_b_proj': _L0_attn_in['b_proj'], 'L0_ffn_router_w': _L0_ffn_in['router_w'], 'L0_ffn_router_b': _L0_ffn_in['router_b'], 'L0_ffn_w1': _L0_ffn_in['w1'], 'L0_ffn_b1': _L0_ffn_in['b1'], 'L0_ffn_w2': _L0_ffn_in['w2'], 'L0_ffn_b2': _L0_ffn_in['b2']}

def reference(x, L0_tok_ln_gamma, L0_tok_ln_beta, L0_tok_W, L0_tok_b, L0_attn_W_attn, L0_attn_b_attn, L0_attn_W_proj, L0_attn_b_proj, L0_ffn_router_w, L0_ffn_router_b, L0_ffn_w1, L0_ffn_b1, L0_ffn_w2, L0_ffn_b2):
    import jax
    import jax.numpy as jnp

    def _L0_tok_ref(x, ln_gamma, ln_beta, W, b):
        import jax, jax.numpy as jnp
        import numpy as np
        PATCH = 4
        SHIFT = PATCH // 2
        EMBED = 192
        PATCH_DIM = 3 * 3 * PATCH * PATCH
        s = SHIFT
        p = PATCH
        xp = jnp.pad(x, ((0, 0), (0, 0), (s, s), (s, s)))
        x_up = xp[..., :-2 * s, s:-s]
        x_left = xp[..., s:-s, :-2 * s]
        out = jnp.concatenate([x, x_up, x_left], axis=1)
        B, C, H, Wd = out.shape
        h, w = (H // p, Wd // p)
        out = out.reshape(B, C, h, p, w, p).transpose(0, 2, 4, 3, 5, 1).reshape(B, h * w, p * p * C)
        mu = jnp.mean(out, axis=-1, keepdims=True)
        var = jnp.var(out, axis=-1, keepdims=True)
        out = (out - mu) * jax.lax.rsqrt(var + 1e-05) * ln_gamma + ln_beta
        return out @ W + b

    def _L0_attn_ref(x, W_attn, b_attn, W_proj, b_proj):
        import jax, jax.numpy as jnp
        import numpy as np
        B, S, D, H = (8, 256, 192, 12)
        HS = D // H
        b, s, d = x.shape
        qkv = (x @ W_attn + b_attn).reshape(b, s, 3, H, HS)
        q, k, v = (qkv[:, :, 0], qkv[:, :, 1], qkv[:, :, 2])
        scale = jnp.sqrt(jnp.asarray(HS, dtype=x.dtype))
        scores = jnp.einsum('bqhd,bkhd->bhqk', q, k) / scale
        causal = jnp.tril(jnp.ones((s, s), dtype=bool))
        scores = jnp.where(causal, scores, -jnp.inf)
        attn = jax.nn.softmax(scores, axis=-1)
        out = jnp.einsum('bhqk,bkhd->bqhd', attn, v).reshape(b, s, H * HS)
        return out @ W_proj + b_proj

    def _L0_ffn_ref(x, router_w, router_b, w1, b1, w2, b2):
        import jax, jax.numpy as jnp
        import numpy as np
        DIM = 192
        HIDDEN = 192
        NUM_EXPERTS = 4
        B, S = (16, 512)
        logits = jnp.einsum('bsd,de->bse', x, router_w) + router_b
        probs = jax.nn.softmax(logits, axis=-1)
        idx = jnp.argmax(probs, axis=-1)
        dispatch = jax.nn.one_hot(idx, NUM_EXPERTS, dtype=x.dtype)
        h = jnp.einsum('bsd,edh->besh', x, w1) + b1[None, :, None, :]
        h = jax.nn.gelu(h, approximate=False)
        y = jnp.einsum('besh,ehd->besd', h, w2) + b2[None, :, None, :]
        out = jnp.einsum('besd,bse->bsd', y, dispatch)
        out = out + x
        return out
    h = _L0_tok_ref(x, L0_tok_ln_gamma, L0_tok_ln_beta, L0_tok_W, L0_tok_b)
    h = h + _L0_attn_ref(_layernorm(h, axis=-1), L0_attn_W_attn, L0_attn_b_attn, L0_attn_W_proj, L0_attn_b_proj)
    h = h + _L0_ffn_ref(_layernorm(h, axis=-1), L0_ffn_router_w, L0_ffn_router_b, L0_ffn_w1, L0_ffn_b1, L0_ffn_w2, L0_ffn_b2)
    return h

_drawn_inputs = setup_inputs


def setup_inputs(seed=0):
    import zlib

    import numpy as np

    out = dict(_drawn_inputs(seed))
    spreads = {'L0_tok_ln_gamma': (1.0, 0.2),
     'L0_tok_ln_beta': (0.0, 0.1),
     'L0_tok_b': (0.0, 0.1),
     'L0_attn_b_attn': (0.0, 0.1),
     'L0_attn_b_proj': (0.0, 0.1)}
    factors = {'L0_ffn_b1': 4.78}
    for name, (base, spread) in spreads.items():
        noise = np.random.default_rng([zlib.crc32(name.encode()), seed]).standard_normal(out[name].shape)
        drawn = base * np.exp(spread * noise) if base else spread * noise
        out[name] = jnp.asarray(drawn.astype(out[name].dtype))
    for name, factor in factors.items():
        out[name] = (out[name] * factor).astype(out[name].dtype)
    return out
```

```python
import concourse.bass as bass
from concourse import mybir
from contextlib import ExitStack


def vit_tower(nc, x, tok_gamma, tok_beta, tok_w, tok_b, w_attn, b_attn, w_proj, b_proj,
              router_w, router_b, w1, b1, w2, b2, out):
    fp32 = mybir.dt.float32
    fp32r = mybir.dt.float32r
    bf16 = mybir.dt.bfloat16
    ALU = mybir.AluOpType
    ACT = mybir.ActivationFunctionType
    AX = mybir.AxisListType

    P = 128
    B, C, IMG, _ = x.shape
    PATCH = 4
    SHIFT = PATCH // 2
    G = IMG // PATCH
    ROWS = C * PATCH
    KINDS = 3
    FK = ROWS * PATCH
    F = KINDS * FK
    FB = F - P
    D = tok_w.shape[1]
    DB = D - P
    S = G * G
    TPB = S // P
    NT = B * TPB
    TOK = B * S
    H = 12
    HS = D // H
    HG = 4
    NG = H // HG
    UNITS = B * NG
    PAIRS = H // 2
    SLOT = 4 * HS
    NE, HID = router_w.shape[1], w1.shape[2]
    NH = NE * HID
    HC = NH // P
    TOK_EPS = 1e-5
    EPS = 1e-5
    SCALE = float(HS) ** -0.5
    MASKED = -1e30
    OFF = float(2 ** 30)

    ctx = ExitStack()
    with ctx:
        def sb(name, shape, dt=fp32):
            return ctx.enter_context(nc.sbuf_tensor(name, shape, dt))

        def sem(name):
            return ctx.enter_context(nc.semaphore(name))

        img = sb("img", [B * G, ROWS, IMG])
        img_up = sb("img_up", [B * G, ROWS, IMG])
        first_up = img_up[0:B, :, :].rearrange("i (c r) w -> i c r w", c=C)
        patches = sb("patches", [B * G, G, F])
        tokens = sb("tokens", [P, NT, F])
        tokw_a = sb("tokw_a", [P, D])
        tokw_b = sb("tokw_b", [FB + 1, D])
        gb_a = sb("gb_a", [P, 2])
        gb_b = sb("gb_b", [FB, 2])
        qkvw_a = sb("qkvw_a", [P, 3 * D])
        qkvw_b = sb("qkvw_b", [DB + 1, 3 * D])
        projw_a = sb("projw_a", [P, D])
        projw_b = sb("projw_b", [DB + 1, D])
        rw_a = sb("rw_a", [P, NE])
        rw_b = sb("rw_b", [DB + 1, NE])
        w1_a = sb("w1_a", [P, NH])
        w1_b = sb("w1_b", [DB + 1, NH])
        w2_sb = sb("w2_sb", [P, HC, D])
        b2_sb = sb("b2_sb", [NE, D])
        ident = sb("ident", [P, P])
        ident_r = sb("ident_r", [P, P], fp32r)
        ident_b = sb("ident_b", [P, P], bf16)
        later = sb("later", [P, P], bf16)
        head_rows = sb("head_rows", [2 * HG, HG, P], bf16)
        expert_rows = sb("expert_rows", [NE, NH], bf16)
        minus_half = sb("minus_half", [P, TPB])
        first_wins = sb("first_wins", [P, TPB, NE])
        stats = sb("stats", [P, NT, 6])
        mv = sb("mv", [P, NT, 2])
        var_eps = sb("var_eps", [P, NT])
        rstd = sb("rstd", [P, NT])
        xn = sb("xn", [P, NT, D])
        xt_a = sb("xt_a", [P, TOK])
        xt_b = sb("xt_b", [DB + 1, TOK])
        ft_a = sb("ft_a", [P, TOK])
        ft_b = sb("ft_b", [FB + 1, TOK])
        at_a = sb("at_a", [P, TOK])
        at_b = sb("at_b", [DB + 1, TOK])
        h = sb("h", [P, NT, D])
        halves = sb("halves", [P, 2, 2 * H, 4, HS], fp32r)
        qk_t = sb("qk_t", [P, 2 * PAIRS, TOK], fp32r)
        v_aug = sb("v_aug", [P, NT, H, 2 * HS])
        neg_max = sb("neg_max", [P, 2, TPB, HG])
        max_parts = sb("max_parts", [P, 2, TPB, 2, HG], bf16)
        max_t = sb("max_t", [2 * HG, 2, S], bf16)
        probs = sb("probs", [P, 2, HG * (S + P)])
        ctx_t = sb("ctx_t", [P, B, NG, S])
        recip = sb("recip", [P, NT, H])
        ctx_n = sb("ctx_n", [P, NT, D])
        logit = sb("logit", [P, NT, NE])
        best = sb("best", [P, NT])
        tie = sb("tie", [P, NT, NE])
        onehot = sb("onehot", [P, NT, NE])
        onehot_t = sb("onehot_t", [NE, TOK])
        others_t = sb("others_t", [NE, TOK], bf16)
        hidden = sb("hidden", [P, B, HC, S])
        skip = sb("skip", [P, NT, D])
        result = sb("result", [P, NT, D])

        big = [ctx.enter_context(nc.psum_tensor(f"big{i}", [P, 3 * 512], fp32)) for i in range(2)]
        small = [ctx.enter_context(nc.psum_tensor(f"small{i}", [P, 512], fp32)) for i in range(2)]

        BIG = []
        for b in range(B):
            for t in (TPB * b, TPB * b + 1):
                BIG += [("qkv", t), ("turn", t)]
        for i in range(UNITS + 1):
            BIG += [("scores", i)] * (i < UNITS) + [("expo", i - 1)] * (i >= 1)
        BIG += [("hidden", b) for b in range(B)]
        SMALL = [[], []]
        for b in range(B):
            for stage in ("tok_t", "tok"):
                for t in (TPB * b, TPB * b + 1):
                    SMALL[t % 2].append((stage, t))
        for t in range(NT):
            SMALL[t % 2].append(("x2_t", t))
        for u in range(UNITS):
            SMALL[0].append(("max_t", u))
            SMALL[1].append(("pv", u))
        for stage in ("ctx", "ctx_t", "proj", "x3_t", "route", "onehot_t", "y"):
            for t in range(NT):
                SMALL[t % 2].append((stage, t))

        def big_use(what):
            n = BIG.index(what)
            return n % 2, n // 2

        def small_use(what):
            w = 0 if what in SMALL[0] else 1
            return w, SMALL[w].index(what)

        img_in, up_in, zero_in = sem("img_in"), sem("up_in"), sem("zero_in")
        pad_done = sem("pad_done")
        patches_done = sem("patches_done")
        tokens_in = [sem(f"tokens_in{t}") for t in range(NT)]
        tokw_in, qkvw_in, projw_in, rw_in = sem("tokw_in"), sem("qkvw_in"), sem("projw_in"), sem("rw_in")
        w1_in, w2_in = sem("w1_in"), sem("w2_in")
        consts = sem("consts")
        idents = sem("idents")
        ones_set = sem("ones_set")
        dve_step = sem("dve_step")
        pool_step = sem("pool_step")
        var_done = sem("var_done")
        rstd_done = sem("rstd_done")
        xn_done = sem("xn_done")
        ft_done, x2t_done, ctxt_done, x3t_done = (sem(n) for n in ("ft_done", "x2t_done", "ctxt_done", "x3t_done"))
        hi_done, lo_done = sem("hi_done"), sem("lo_done")
        turned = sem("turned")
        max_split = sem("max_split")
        maxt_done = sem("maxt_done")
        exp_done = sem("exp_done")
        causal_done = sem("causal_done")
        pv_out = sem("pv_out")
        even_scores, even_shifted = sem("even_scores"), sem("even_shifted")
        ctxn_done = sem("ctxn_done")
        onehot_done, onehott_done = sem("onehot_done"), sem("onehott_done")
        hidden_done = sem("hidden_done")
        skip_done = sem("skip_done")
        result_done = sem("result_done")
        out_done = sem("out_done")
        big_full = [sem(f"big_full{i}") for i in range(2)]
        small_full = [sem(f"small_full{i}") for i in range(2)]
        h_in, h_out, logit_in, max_done = sem("h_in"), sem("h_out"), sem("logit_in"), sem("max_done")

        block = ctx.enter_context(nc.Block())

        def cols(t):
            return slice(P * t, P * t + P)

        @block.sync
        def _(sp):
            x_rows = x.rearrange("b c (i r) w -> b i c (r w)", r=PATCH)
            for b in range(B):
                sp.dma_start(img[b:B * G:B, :, :].rearrange("i (c r) w -> i c (r w)", c=C),
                             x_rows[b]).then_inc(img_in, 16)
            planes = tok_w.rearrange("(q c) n -> c q n", c=F // 16)
            for c in range(F // 16):
                dst = tokw_a[16 * c:16 * c + 16, :] if 16 * c < P else tokw_b[0:FB, :]
                sp.dma_start(dst, planes[c]).then_inc(tokw_in, 16)
            sp.wait_ge(patches_done, 4)
            for t in range(NT):
                i0 = B * (G // TPB) * (t % TPB) + t // TPB
                sp.dma_start(tokens[:, t, :],
                             patches[i0:i0 + B * (G // TPB) - 1:B, :, :]).then_inc(tokens_in[t], 16)
            for t in range(NT):
                sp.wait_ge(result_done, t + 1)
                sp.dma_start(out[t // TPB, cols(t % TPB), :], result[:, t, :]).then_inc(out_done, 16)
            sp.wait_ge(out_done, 16 * NT)

        @block.gpsimd
        def _(pool):
            step = [0]

            def link(ins):
                step[0] += 1
                ins.then_inc(pool_step, 1)
                pool.wait_ge(pool_step, step[0])

            link(nc.gpsimd.memset(ident[:], 0.0))
            link(nc.gpsimd.affine_select(out=ident[:], in_=ident[:], compare_op=ALU.not_equal, fill=1.0,
                                         base=0, pattern=[[-1, P]], channel_multiplier=1))
            nc.gpsimd.tensor_copy(ident_b[:], ident[:]).then_inc(idents, 1)
            link(nc.gpsimd.memset(minus_half[:], -0.5))
            link(nc.gpsimd.memset(later[:], 0.0))
            nc.gpsimd.affine_select(out=later[:], in_=later[:], compare_op=ALU.is_ge, fill=MASKED,
                                    base=0, pattern=[[-1, P]], channel_multiplier=1).then_inc(consts, 1)
            link(nc.gpsimd.memset(head_rows[:], 0.0))
            link(nc.gpsimd.affine_select(out=head_rows[:], in_=head_rows[:], compare_op=ALU.not_equal,
                                         fill=1.0, base=0, pattern=[[-1, HG], [0, P]], channel_multiplier=1))
            nc.gpsimd.affine_select(out=head_rows[:], in_=head_rows[:], compare_op=ALU.not_equal,
                                    fill=1.0, base=-HG, pattern=[[-1, HG], [0, P]],
                                    channel_multiplier=1).then_inc(consts, 1)
            link(nc.gpsimd.memset(expert_rows[:], 0.0))
            ev = expert_rows[:].rearrange("e (f n) -> e f n", f=NE)
            nc.gpsimd.affine_select(out=ev, in_=ev, compare_op=ALU.not_equal, fill=OFF, base=0,
                                    pattern=[[-1, NE], [0, HID]], channel_multiplier=1).then_inc(consts, 1)
            for e in range(NE):
                link(nc.gpsimd.memset(first_wins[:, :, e:e + 1], float(NE - e)))
            nc.gpsimd.memset(v_aug[:], 1.0).then_inc(consts, 1)
            pool.dma_start(projw_a[:], w_proj[0:P, :]).then_inc(projw_in, 16)
            pool.dma_start(projw_b[0:DB, :], w_proj[P:D, :]).then_inc(projw_in, 16)
            pool.dma_start(projw_b[DB:DB + 1, :], b_proj.rearrange("(a n) -> a n", a=1)).then_inc(projw_in, 16)
            pool.dma_start(rw_a[:], router_w[0:P, :]).then_inc(rw_in, 16)
            pool.dma_start(rw_b[0:DB, :], router_w[P:D, :]).then_inc(rw_in, 16)
            pool.dma_start(rw_b[DB:DB + 1, :], router_b.rearrange("(a n) -> a n", a=1)).then_inc(rw_in, 16)
            w1_v = w1.rearrange("e d n -> d e n")
            pool.dma_start(w1_a[:].rearrange("d (e n) -> d e n", e=NE), w1_v[0:P]).then_inc(w1_in, 16)
            pool.dma_start(w1_b[0:DB, :].rearrange("d (e n) -> d e n", e=NE), w1_v[P:D]).then_inc(w1_in, 16)
            pool.dma_start(w1_b[DB:DB + 1, :], b1.rearrange("e (a n) -> a (e n)", a=1)).then_inc(w1_in, 16)
            pool.dma_start(w2_sb[:], w2.rearrange("e n d -> (e n) d").rearrange("(c p) d -> p c d", p=P))\
                .then_inc(w2_in, 16)
            pool.dma_start(b2_sb[:], b2).then_inc(w2_in, 16)

            n_rstd = [0]

            def rstds(b):
                n_rstd[0] += 1
                pool.wait_ge(var_done, n_rstd[0])
                s = slice(TPB * b, TPB * b + TPB)
                nc.gpsimd.tensor_tensor(rstd[:, s], var_eps[:, s], minus_half[:], ALU.pow).then_inc(rstd_done, 1)

            def causal(u):
                pool.wait_ge(exp_done, u + 1)
                on = probs[:, u % 2, 0:HG * S].rearrange("p (g q) -> p g q", g=HG)[:, :, 0:P]
                off = probs[:, u % 2, HG * S:].rearrange("p (g q) -> p g q", g=HG)
                for blk in (on, off):
                    nc.gpsimd.affine_select(out=blk, in_=blk, compare_op=ALU.is_ge, fill=0.0, base=0,
                                            pattern=[[0, HG], [1, P]], channel_multiplier=-1)\
                        .then_inc(causal_done, 1)

            rstds(0)
            rstds(1)
            rstds(0)
            rstds(1)
            for u in range(UNITS):
                causal(u)
            rstds(0)
            rstds(1)
            for t in range(NT):
                if t % TPB == 0:
                    pool.wait_ge(xn_done, 2 * NT + t + TPB)
                nc.gpsimd.tensor_tensor(skip[:, t, :], h[:, t, :], xn[:, t, :], ALU.add).then_inc(skip_done, 1)

        @block.scalar
        def _(act):
            for b in range(B):
                rows = x[b, :, SHIFT:IMG - SHIFT, :].rearrange("c (i r) w -> i c (r w)", r=PATCH)
                act.dma_start(img_up[B + b:B * G:B, :, :].rearrange("i (c r) w -> i c (r w)", c=C),
                              rows).then_inc(up_in, 16)
            act.dma_start(first_up[:, :, SHIFT:PATCH, :], x[:, :, 0:SHIFT, :]).then_inc(up_in, 16)
            with nc.allow_non_contiguous_dma(reason="two small vectors"):
                for n, vec in enumerate((tok_gamma, tok_beta)):
                    planes = vec.rearrange("(q c a) -> c q a", c=F // 16, a=1)
                    for c in range(F // 16):
                        dst = gb_a[16 * c:16 * c + 16, n:n + 1] if 16 * c < P else gb_b[0:FB, n:n + 1]
                        act.dma_start(dst, planes[c]).then_inc(tokw_in, 16)
            act.dma_start(tokw_b[FB:FB + 1, :], tok_b.rearrange("(a n) -> a n", a=1)).then_inc(tokw_in, 16)
            act.dma_start(qkvw_a[:], w_attn[0:P, :]).then_inc(qkvw_in, 16)
            act.dma_start(qkvw_b[0:DB, :], w_attn[P:D, :]).then_inc(qkvw_in, 16)
            act.dma_start(qkvw_b[DB:DB + 1, :], b_attn.rearrange("(a n) -> a n", a=1)).then_inc(qkvw_in, 16)

            def small_in(what):
                w, n = small_use(what)
                act.wait_ge(small_full[w], n + 1)
                return w

            def tok_turned(t):
                w = small_in(("tok_t", t))
                nc.scalar.activation(ft_a[:, cols(t)], small[w][:, 0:P], ACT.Identity, bias=gb_a[:, 1:2],
                                     scale=gb_a[:, 0:1]).then_inc(ft_done, 1)
                nc.scalar.activation(ft_b[0:FB, cols(t)], small[w][0:FB, P:2 * P], ACT.Identity,
                                     bias=gb_b[:, 1:2], scale=gb_b[:, 0:1]).then_inc(ft_done, 1)

            def turned_copy(what, dst_a, dst_b, done):
                w = small_in(what)
                t = what[1]
                nc.scalar.activation(dst_a[:, cols(t)], small[w][:, 0:P], ACT.Copy).then_inc(done, 1)
                nc.scalar.activation(dst_b[0:DB, cols(t)], small[w][0:DB, P:2 * P], ACT.Copy).then_inc(done, 1)

            def split_high(t):
                a, n = big_use(("qkv", t))
                act.wait_ge(big_full[a], n + 1)
                if t >= 2:
                    a2, n2 = big_use(("turn", t - 2))
                    act.wait_ge(big_full[a2], n2 + 1)
                q = big[a][:, 0:D].rearrange("p (n d) -> p n d", n=H)
                k = big[a][:, D:2 * D].rearrange("p (n d) -> p n d", n=H)
                for j in range(2):
                    nc.scalar.activation(halves[:, t % 2, 0:H, j, :], q, ACT.Copy).then_inc(hi_done, 1)
                    nc.scalar.activation(halves[:, t % 2, H:2 * H, 2 * j, :], k, ACT.Copy).then_inc(hi_done, 1)
                v = big[a][:, 512:512 + D].rearrange("p (n d) -> p n d", n=H)
                act.wait_ge(consts, 4)
                nc.scalar.activation(v_aug[:, t, :, 0:HS], v, ACT.Copy).then_inc(hi_done, 1)

            def turned_halves(t):
                a, n = big_use(("turn", t))
                act.wait_ge(big_full[a], n + 1)
                nc.scalar.activation(qk_t[:, 0:8, cols(t)],
                                     big[a][:, 0:2 * 512].rearrange("p (n q) -> p n q", n=8),
                                     ACT.Copy).then_inc(turned, 1)

            def max_rows(u):
                w = small_in(("max_t", u))
                if u >= 2:
                    a, n = big_use(("expo", u - 2))
                    act.wait_ge(big_full[a], n + 1)
                src = small[w][0:2 * HG, 0:P].bitcast(bf16)
                nc.scalar.activation(max_t[:, u % 2, :], src, ACT.Copy).then_inc(maxt_done, 1)

            def exps(u):
                a, n = big_use(("expo", u))
                act.wait_ge(big_full[a], n + 1)
                if u >= 2:
                    w, m = small_use(("pv", u - 2))
                    act.wait_ge(small_full[w], m + 1)
                nc.scalar.activation(probs[:, u % 2, :], big[a][:, :], ACT.Exp, scale=SCALE).then_inc(exp_done, 1)

            def gelu(b):
                a, n = big_use(("hidden", b))
                act.wait_ge(big_full[a], n + 1)
                nc.scalar.activation(hidden[:, b, :, :], big[a][:, :].rearrange("p (c q) -> p c q", c=HC),
                                     ACT.Gelu).then_inc(hidden_done, 1)

            act.wait_ge(tokw_in, 16 * (3 * (F // 16) + 1))
            for t in range(NT):
                tok_turned(t)
            act.wait_ge(ones_set, 3)
            for t in range(NT):
                turned_copy(("x2_t", t), xt_a, xt_b, x2t_done)
            for t in range(NT):
                split_high(t)
                turned_halves(t)
            for u in range(UNITS):
                max_rows(u)
                exps(u)
            for t in range(NT):
                turned_copy(("ctx_t", t), at_a, at_b, ctxt_done)
            for t in range(NT):
                turned_copy(("x3_t", t), xt_a, xt_b, x3t_done)
            for b in range(B):
                gelu(b)

        @block.vector
        def _(dve):
            step = [0]

            def link(ins):
                step[0] += 1
                ins.then_inc(dve_step, 1)
                dve.wait_ge(dve_step, step[0])

            def small_in(what):
                w, n = small_use(what)
                dve.wait_ge(small_full[w], n + 1)
                return w

            def big_in(what):
                a, n = big_use(what)
                dve.wait_ge(big_full[a], n + 1)
                return a

            nc.vector.memset(first_up[:, :, 0:SHIFT, :], 0.0).then_inc(zero_in, 1)
            nc.vector.memset(patches[:, 0, 2 * FK:3 * FK], 0.0).then_inc(pad_done, 1)
            nc.vector.memset(ft_b[:], 1.0).then_inc(ones_set, 1)
            nc.vector.memset(xt_b[DB:DB + 1, :], 1.0).then_inc(ones_set, 1)
            nc.vector.memset(at_b[DB:DB + 1, :], 1.0).then_inc(ones_set, 1)
            dve.wait_ge(idents, 1)
            nc.vector.tensor_copy(ident_r[:], ident[:]).then_inc(idents, 1)

            def patch_view(k, j0=0):
                return patches[:, j0:G, FK * k:FK * k + FK].rearrange("p j (r c) -> p j r c", c=PATCH)

            dve.wait_ge(img_in, 16 * B)
            nc.vector.tensor_copy(patch_view(0), img[:].rearrange("p r (j c) -> p j r c", c=PATCH))\
                .then_inc(patches_done, 1)
            nc.vector.tensor_copy(
                patch_view(2, 1),
                img[:, :, SHIFT:IMG - SHIFT].rearrange("p r (j c) -> p j r c", c=PATCH)).then_inc(patches_done, 1)
            dve.wait_ge(pad_done, 1)
            nc.vector.tensor_copy(patch_view(2)[:, 0, :, SHIFT:PATCH], img[:, :, 0:SHIFT]).then_inc(patches_done, 1)
            dve.wait_ge(up_in, 16 * (B + 1))
            dve.wait_ge(zero_in, 1)
            nc.vector.tensor_copy(patch_view(1), img_up[:].rearrange("p r (j c) -> p j r c", c=PATCH))\
                .then_inc(patches_done, 1)

            n_rstd = [0]

            def normalise(src, b, eps, width):
                ts = range(TPB * b, TPB * b + TPB)
                for t in ts:
                    last = nc.vector.bn_stats(stats[:, t, :], src(t))
                    if t < ts[-1]:
                        last.then_inc(dve_step, 1)
                        step[0] += 1
                link(last)
                for t in ts:
                    last = nc.vector.bn_aggr(mv[:, t, :], stats[:, t, :])
                    if t < ts[-1]:
                        last.then_inc(dve_step, 1)
                        step[0] += 1
                link(last)
                nc.vector.tensor_scalar(var_eps[:, ts[0]:ts[-1] + 1], mv[:, ts[0]:ts[-1] + 1, 1], eps, None,
                                        ALU.add).then_inc(var_done, 1)
                n_rstd[0] += 1
                dve.wait_ge(rstd_done, n_rstd[0])
                for t in ts:
                    nc.vector.tensor_scalar(xn[:, t, 0:width], src(t), mv[:, t, 0:1], rstd[:, t:t + 1],
                                            ALU.subtract, ALU.mult).then_inc(xn_done, 1)

            def split_low(t):
                a = big_in(("qkv", t))
                dve.wait_ge(hi_done, 5 * t + 5)
                q = big[a][:, 0:D].rearrange("p (n d) -> p n d", n=H)
                k = big[a][:, D:2 * D].rearrange("p (n d) -> p n d", n=H)
                for j in range(2):
                    nc.vector.tensor_tensor(halves[:, t % 2, 0:H, 2 + j, :], q,
                                            halves[:, t % 2, 0:H, 0, :].bitcast(fp32), ALU.subtract)\
                        .then_inc(lo_done, 1)
                    nc.vector.tensor_tensor(halves[:, t % 2, H:2 * H, 1 + 2 * j, :], k,
                                            halves[:, t % 2, H:2 * H, 0, :].bitcast(fp32), ALU.subtract)\
                        .then_inc(lo_done, 1)

            def turned_halves(t):
                a = big_in(("turn", t))
                nc.vector.tensor_copy(qk_t[:, 8:2 * PAIRS, cols(t)],
                                      big[a][:, 2 * 512:3 * 512].rearrange("p (n q) -> p n q", n=4))\
                    .then_inc(turned, 1)

            def maxima(u):
                a = big_in(("scores", u))
                if u >= 2:
                    w, n = small_use(("max_t", u - 2))
                    dve.wait_ge(small_full[w], n + 1)
                p = u % 2
                nc.vector.tensor_reduce(neg_max[:, p, 0, :],
                                        big[a][:, 2 * 512:3 * 512].rearrange("p (g k) -> p g k", g=HG),
                                        AX.X, ALU.max, negate=True).then_inc(max_done, 1)
                nc.vector.tensor_reduce(neg_max[:, p, 1, :],
                                        big[a][:, 0:2 * 512].rearrange("p (g k) -> p g k", g=HG),
                                        AX.X, ALU.max, negate=True).then_inc(max_done, 1)
                dve.wait_ge(max_done, 2 * u + 2)
                link(nc.vector.tensor_copy(max_parts[:, p, :, 0, :], neg_max[:, p, :, :]))
                nc.vector.tensor_tensor(max_parts[:, p, :, 1, :], neg_max[:, p, :, :],
                                        max_parts[:, p, :, 0, :], ALU.subtract).then_inc(max_split, 1)

            def pv_copy(u):
                w = small_in(("pv", u))
                nc.vector.tensor_copy(ctx_t[:, u // NG, u % NG, :], small[w][:, 0:S]).then_inc(pv_out, 1)

            def context(t):
                w = small_in(("ctx", t))
                acc = small[w][:, 0:NG * P].rearrange("p (n d) -> p n d", n=H)
                link(nc.vector.reciprocal(recip[:, t, :], acc[:, :, HS]))
                ins = nc.vector.tensor_tensor(
                    ctx_n[:, t, :].rearrange("p (n d) -> p n d", n=H), acc[:, :, 0:HS],
                    recip[:, t, :].unsqueeze(2).to_broadcast([P, H, HS]), ALU.mult)
                ins.then_inc(ctxn_done, 1)

            def attention_out(t):
                w = small_in(("proj", t))
                nc.vector.tensor_tensor(h[:, t, :], small[w][:, 0:D], h[:, t, :], ALU.add).then_inc(h_out, 1)
                dve.wait_ge(h_out, t + 1)

            def route(t):
                w = small_in(("route", t))
                nc.vector.tensor_copy(logit[:, t, :], small[w][:, 0:NE]).then_inc(logit_in, 1)
                dve.wait_ge(logit_in, t + 1)
                link(nc.vector.tensor_reduce(best[:, t:t + 1], logit[:, t, :], AX.X, ALU.max))
                link(nc.vector.scalar_tensor_tensor(out=tie[:, t, :], in0=logit[:, t, :], scalar=best[:, t:t + 1],
                                                    in1=first_wins[:, 0, :], op0=ALU.is_equal, op1=ALU.mult))
                link(nc.vector.tensor_reduce(best[:, t:t + 1], tie[:, t, :], AX.X, ALU.max))
                nc.vector.tensor_scalar(onehot[:, t, :], tie[:, t, :], best[:, t:t + 1], None,
                                        ALU.is_equal).then_inc(onehot_done, 1)

            def onehot_rows(t):
                w = small_in(("onehot_t", t))
                nc.vector.tensor_copy(onehot_t[:, cols(t)], small[w][0:NE, 0:P]).then_inc(onehott_done, 1)
                nc.vector.tensor_scalar(others_t[:, cols(t)], small[w][0:NE, 0:P], 1.0, None,
                                        ALU.subtract).then_inc(onehott_done, 1)

            def last_sum(t):
                w = small_in(("y", t))
                dve.wait_ge(skip_done, t + 1)
                nc.vector.tensor_tensor(result[:, t, :], small[w][:, 0:D], skip[:, t, :],
                                        ALU.add).then_inc(result_done, 1)

            for b in range(B):
                for t in (TPB * b, TPB * b + 1):
                    dve.wait_ge(tokens_in[t], 16)
                normalise(lambda t: tokens[:, t, :], b, TOK_EPS, F)
            for b in range(B):
                for t in (TPB * b, TPB * b + 1):
                    w = small_in(("tok", t))
                    nc.vector.tensor_copy(h[:, t, :], small[w][:, 0:D]).then_inc(h_in, 1)
                    dve.wait_ge(h_in, t + 1)
                normalise(lambda t: h[:, t, :], b, EPS, D)
            for t in range(NT):
                split_low(t)
                turned_halves(t)
            for i in range(UNITS + 2):
                if i < UNITS:
                    maxima(i)
                if i >= 2:
                    pv_copy(i - 2)
            for t in range(NT):
                context(t)
            for b in range(B):
                for t in (TPB * b, TPB * b + 1):
                    attention_out(t)
                normalise(lambda t: h[:, t, :], b, EPS, D)
            for t in range(NT):
                route(t)
            for t in range(NT):
                onehot_rows(t)
            for t in range(NT):
                last_sum(t)

        @block.tensor
        def _(pe):
            def read_by(what):
                stage, n = what
                return {
                    "tok_t": (ft_done, 2 * n + 2), "tok": (h_in, n + 1), "x2_t": (x2t_done, 2 * n + 2),
                    "qkv": (lo_done, 4 * n + 4), "turn": (turned, 2 * n + 2),
                    "scores": (max_done, 2 * n + 2), "max_t": (maxt_done, n + 1),
                    "expo": (exp_done, n + 1), "pv": (pv_out, n + 1),
                    "ctx": (ctxn_done, n + 1), "ctx_t": (ctxt_done, 2 * n + 2), "proj": (h_out, n + 1),
                    "x3_t": (x3t_done, 2 * n + 2), "route": (logit_in, n + 1),
                    "onehot_t": (onehott_done, 2 * n + 2), "hidden": (hidden_done, n + 1),
                    "y": (result_done, n + 1),
                }[stage]

            def ready(what):
                w, n = small_use(what)
                if n:
                    pe.wait_ge(*read_by(SMALL[w][n - 1]))
                return w

            def big_ready(what):
                a, n = big_use(what)
                if n:
                    pe.wait_ge(*read_by(BIG[2 * (n - 1) + a]))
                return a

            def mm(o, l, r, start=True, stop=True, **k):
                return nc.tensor.matmul(o, l, r, start=start, stop=stop, **k)

            def turn(what, src, width):
                w = ready(what)
                nc.tensor.transpose(small[w][:, 0:P], src[:, 0:P], ident[:])
                nc.tensor.transpose(small[w][0:width - P, P:2 * P], src[:, P:width], ident[:])\
                    .then_inc(small_full[w], 1)

            def rows_out(what, xa, xb, wa, wb, width):
                w = ready(what)
                t = what[1]
                mm(small[w][:, 0:width], xa[:, cols(t)], wa, stop=False)
                mm(small[w][:, 0:width], xb[:, cols(t)], wb, start=False).then_inc(small_full[w], 1)

            def qkv(t):
                a = big_ready(("qkv", t))
                pe.wait_ge(x2t_done, 2 * t + 2)
                for o, c0, c1 in ((0, 0, 2 * D), (512, 2 * D, 3 * D)):
                    mm(big[a][:, o:o + c1 - c0], xt_a[:, cols(t)], qkvw_a[:, c0:c1], stop=False)
                    last = mm(big[a][:, o:o + c1 - c0], xt_b[:, cols(t)], qkvw_b[:, c0:c1], start=False)
                last.then_inc(big_full[a], 1)

            def turn_halves(t):
                a = big_ready(("turn", t))
                pe.wait_ge(lo_done, 4 * t + 4)
                pe.wait_ge(hi_done, 5 * t + 5)
                for n in range(2 * PAIRS):
                    last = nc.tensor.transpose(
                        big[a][:, P * n:P * n + P].bitcast(fp32r),
                        halves[:, t % 2, 2 * n:2 * n + 2, :, :].rearrange("p n s d -> p (n s d)"), ident_r[:])
                last.then_inc(big_full[a], 1)

            def qk(hd, which, b, c0, c1):
                r = SLOT * (hd % 2)
                return qk_t[r:r + SLOT, PAIRS * which + hd // 2, S * b + c0:S * b + c1]

            def scores(u):
                a = big_ready(("scores", u))
                b, g = u // NG, u % NG
                areas = [(big[a][:, 0:512].rearrange("p (g k) -> p g k", g=2), S, P),
                         (big[a][:, 512:1024].rearrange("p (g k) -> p g k", g=2), S, P),
                         (big[a][:, 1024:1536].rearrange("p (g k) -> p g k", g=HG), P, 0)]
                for area, width, q0 in areas:
                    mm(area[:, :, width - P:width], ident_b[:],
                       later[:].unsqueeze(1).to_broadcast([P, 512 // width, P]), skip_group_check=True)
                for n, k0, odd in ((2, 0, 0), (0, 0, 0), (1, 0, 1), (2, 2, 1)):
                    area, width, q0 = areas[n]
                    if (n, odd) == (2, 1):
                        pe.wait_ge(even_scores, u + 1)
                    for j in range(2):
                        hd = HG * g + 2 * j + odd
                        last = mm(area[:, k0 + j, :], qk(hd, 0, b, q0, q0 + P), qk(hd, 1, b, 0, width),
                                  start=False, skip_group_check=True)
                    if (n, odd) == (2, 0):
                        last.then_inc(even_scores, 1)
                last.then_inc(big_full[a], 1)

            def max_rows(u):
                w = ready(("max_t", u))
                pe.wait_ge(max_split, u + 1)
                for i in range(TPB):
                    last = nc.tensor.transpose(
                        small[w][0:2 * HG, 64 * i:64 * i + 64].bitcast(bf16),
                        max_parts[:, u % 2, i, :, :].rearrange("p s g -> p (s g)"), ident_b[:])
                last.then_inc(small_full[w], 1)

            def shifted_scores(u):
                a = big_ready(("expo", u))
                b, g = u // NG, u % NG
                pe.wait_ge(maxt_done, u + 1)

                def place(j, k0):
                    c = (512 * (j % 2) + S * (j // 2)) if k0 == 0 else 1024 + P * (2 * (j % 2) + j // 2)
                    return big[a][:, c:c + S - k0]

                for k0 in (0, P):
                    for j in (0, 2, 1, 3):
                        first = j < 2 if k0 == 0 else j == 0
                        mm(place(j, k0), head_rows[:, 2 * (j % 2) + j // 2, :], max_t[:, u % 2, k0:S], start=first,
                           skip_group_check=True)
                for k0, js in ((P, (0, 2)), (0, (0, 2)), (0, (1, 3)), (P, (1, 3))):
                    if (k0, js[0]) == (P, 1):
                        pe.wait_ge(even_shifted, u + 1)
                    for j in js:
                        hd = HG * g + j
                        last = mm(place(j, k0), qk(hd, 1, b, k0, k0 + P), qk(hd, 0, b, k0, S),
                                  start=False, skip_group_check=True)
                    if (k0, js[0]) == (P, 0):
                        last.then_inc(even_shifted, 1)
                last.then_inc(big_full[a], 1)

            def values(u):
                w = ready(("pv", u))
                b, g = u // NG, u % NG
                pe.wait_ge(causal_done, 2 * u + 2)
                for k, (o, q0) in enumerate(((0, 0), (HG * S, P))):
                    for j in range(HG):
                        n = 2 * (j % 2) + j // 2
                        pr = probs[:, u % 2, o + (S - q0) * n:o + (S - q0) * (n + 1)]
                        last = mm(small[w][32 * j:32 * j + 32, q0:S], v_aug[:, TPB * b + k, HG * g + j, :], pr,
                                  start=(k == 0), stop=(k == 1), skip_group_check=True)
                last.then_inc(small_full[w], 1)

            def context_rows(t):
                w = ready(("ctx", t))
                b = t // TPB
                pe.wait_ge(pv_out, NG * (b + 1))
                for g in range(NG):
                    last = nc.tensor.transpose(small[w][:, P * g:P * g + P], ctx_t[:, b, g, cols(t % TPB)], ident[:])
                last.then_inc(small_full[w], 1)

            def hidden_in(b):
                a = big_ready(("hidden", b))
                pe.wait_ge(onehott_done, 2 * TPB * (b + 1))
                s = slice(S * b, S * b + S)
                for c in range(HC):
                    o = big[a][:, S * c:S * c + S]
                    mm(o, expert_rows[:, P * c:P * c + P], others_t[:, s], stop=False)
                    mm(o, w1_a[:, P * c:P * c + P], xt_a[:, s], start=False, stop=False)
                    last = mm(o, w1_b[:, P * c:P * c + P], xt_b[:, s], start=False)
                last.then_inc(big_full[a], 1)

            def experts_out(t):
                w = ready(("y", t))
                b = t // TPB
                pe.wait_ge(hidden_done, b + 1)
                mm(small[w][:, 0:D], onehot_t[:, cols(t)], b2_sb[:], stop=False)
                for c in range(HC):
                    last = mm(small[w][:, 0:D], hidden[:, b, c, cols(t % TPB)], w2_sb[:, c, :],
                              start=False, stop=(c == HC - 1))
                last.then_inc(small_full[w], 1)

            pe.wait_ge(idents, 2)
            pe.wait_ge(consts, 4)
            pe.wait_ge(ones_set, 3)
            for b in range(B):
                for t in (TPB * b, TPB * b + 1):
                    pe.wait_ge(xn_done, t + 1)
                    turn(("tok_t", t), xn[:, t, :], F)
                for t in (TPB * b, TPB * b + 1):
                    pe.wait_ge(ft_done, 2 * t + 2)
                    rows_out(("tok", t), ft_a, ft_b, tokw_a[:], tokw_b[:], D)
            for t in range(NT):
                pe.wait_ge(xn_done, NT + t + 1)
                turn(("x2_t", t), xn[:, t, :], D)
            pe.wait_ge(qkvw_in, 16 * 3)
            for t in range(NT):
                qkv(t)
                turn_halves(t)
            pe.wait_ge(turned, 2 * NT)
            for i in range(UNITS + 2):
                if i < UNITS:
                    scores(i)
                if 1 <= i <= UNITS:
                    max_rows(i - 1)
                    shifted_scores(i - 1)
                if i >= 2:
                    values(i - 2)
            for t in range(NT):
                context_rows(t)
            for t in range(NT):
                pe.wait_ge(ctxn_done, t + 1)
                turn(("ctx_t", t), ctx_n[:, t, :], D)
            pe.wait_ge(projw_in, 16 * 3)
            for t in range(NT):
                pe.wait_ge(ctxt_done, 2 * t + 2)
                rows_out(("proj", t), at_a, at_b, projw_a[:], projw_b[:], D)
            for t in range(NT):
                pe.wait_ge(xn_done, 2 * NT + t + 1)
                turn(("x3_t", t), xn[:, t, :], D)
            pe.wait_ge(rw_in, 16 * 3)
            for t in range(NT):
                pe.wait_ge(x3t_done, 2 * t + 2)
                rows_out(("route", t), xt_a, xt_b, rw_a[:], rw_b[:], NE)
            for t in range(NT):
                w = ready(("onehot_t", t))
                pe.wait_ge(onehot_done, t + 1)
                nc.tensor.transpose(small[w][0:NE, 0:P], onehot[:, t, :], ident[:]).then_inc(small_full[w], 1)
            pe.wait_ge(w1_in, 16 * 3)
            for b in range(B):
                hidden_in(b)
            pe.wait_ge(w2_in, 16 * 2)
            for t in range(NT):
                experts_out(t)


_INS = ['x', 'L0_tok_ln_gamma', 'L0_tok_ln_beta', 'L0_tok_W', 'L0_tok_b', 'L0_attn_W_attn', 'L0_attn_b_attn',
        'L0_attn_W_proj', 'L0_attn_b_proj', 'L0_ffn_router_w', 'L0_ffn_router_b', 'L0_ffn_w1', 'L0_ffn_b1',
        'L0_ffn_w2', 'L0_ffn_b2']


def kernel(**inputs):
    import numpy as _np
    import concourse.bacc as _bacc
    from concourse import mybir as _mybir
    from concourse.bass_utils import run_bass_kernel_spmd as _run

    nc = _bacc.Bacc("TRN2", target_bir_lowering=False, num_devices=1)
    arrays, args = {}, []
    for name in _INS:
        a = _np.ascontiguousarray(inputs[name])
        arrays[f"in_{name}_dram"] = a
        args.append(nc.dram_tensor(f"in_{name}_dram", a.shape, _mybir.dt.from_np(a.dtype), kind="ExternalInput").ap())
    out = nc.dram_tensor("out_dram", (2, 256, 192), _mybir.dt.float32, kind="ExternalOutput").ap()
    vit_tower(nc, *args, out)
    r = _run(nc, [arrays], core_ids=[0])
    return r.results[0]["out_dram"]
```

```python
import concourse.bass as bass
from concourse import mybir
from contextlib import ExitStack


def vit_tower(nc, x, tok_gamma, tok_beta, tok_w, tok_b, w_attn, b_attn, w_proj, b_proj,
              router_w, router_b, w1, b1, w2, b2, out):
    fp32 = mybir.dt.float32
    fp32r = mybir.dt.float32r
    bf16 = mybir.dt.bfloat16
    ALU = mybir.AluOpType
    ACT = mybir.ActivationFunctionType
    AX = mybir.AxisListType

    P = 128
    B, C, IMG, _ = x.shape
    PATCH = 4
    SHIFT = PATCH // 2
    G = IMG // PATCH
    ROWS = C * PATCH
    KINDS = 3
    FK = ROWS * PATCH
    F = KINDS * FK
    FB = F - P
    D = tok_w.shape[1]
    DB = D - P
    S = G * G
    TPB = S // P
    NT = B * TPB
    TOK = B * S
    H = 12
    HS = D // H
    HG = 4
    NG = H // HG
    UNITS = B * NG
    PAIRS = H // 2
    SLOT = 4 * HS
    NE, HID = router_w.shape[1], w1.shape[2]
    NH = NE * HID
    HC = NH // P
    TOK_EPS = 1e-5
    EPS = 1e-5
    SCALE = float(HS) ** -0.5
    MASKED = -1e30
    START = (36,)
    FILL = {"tok_t": (0, 4, 0, 2), "tok": (0, 0, 0, 4), "x2_t": (0, 2)}
    STEADY = {("x2_t", 2): (("x2_t", 2), 1), ("turn", 1): (("max_t", 0), 2), ("scores", 0): (("max_t", 0), 6),
              ("max_t", 0): (("pv", 0), 5), ("turn", 3): (("pv", 0), 5), ("pv", 1): (("pv", 1), 6)}
    OFF = float(2 ** 30)

    ctx = ExitStack()
    with ctx:
        def sb(name, shape, dt=fp32):
            return ctx.enter_context(nc.sbuf_tensor(name, shape, dt))

        def sem(name):
            return ctx.enter_context(nc.semaphore(name))

        img = sb("img", [B * G, ROWS, IMG])
        img_up = sb("img_up", [B * G, ROWS, IMG])
        first_up = img_up[0:B, :, :].rearrange("i (c r) w -> i c r w", c=C)
        patches = sb("patches", [B * G, G, F])
        tokens = sb("tokens", [P, NT, F])
        tokw_a = sb("tokw_a", [P, D])
        tokw_b = sb("tokw_b", [FB + 1, D])
        gb_a = sb("gb_a", [P, 2])
        gb_b = sb("gb_b", [FB, 2])
        qkvw_a = sb("qkvw_a", [P, 3 * D])
        qkvw_b = sb("qkvw_b", [DB + 1, 3 * D])
        projw = sb("projw", [P, NG, D])
        rw_a = sb("rw_a", [P, NE])
        rw_b = sb("rw_b", [DB + 1, NE])
        w1_a = sb("w1_a", [P, NH])
        w1_b = sb("w1_b", [DB + 1, NH])
        w2_sb = sb("w2_sb", [P, HC, D])
        b2_sb = sb("b2_sb", [NE, D])
        ident = sb("ident", [P, P])
        ident_r = sb("ident_r", [P, P], fp32r)
        ident_b = sb("ident_b", [P, P], bf16)
        later = sb("later", [P, P], bf16)
        head_rows = sb("head_rows", [2 * HG, HG, P], bf16)
        expert_rows = sb("expert_rows", [NE, NH], bf16)
        ones = sb("ones", [P, 2 * HS])
        warm = sb("warm", [P, 512], bf16)
        first_act = sb("first_act", [P, 1])
        minus_half = sb("minus_half", [P, TPB])
        first_wins = sb("first_wins", [P, TPB, NE])
        stats = sb("stats", [P, NT, 6])
        mv = sb("mv", [P, NT, 2])
        var_eps = sb("var_eps", [P, NT])
        rstd = sb("rstd", [P, NT])
        xn = sb("xn", [P, NT, D])
        xt_a = sb("xt_a", [P, TOK])
        xt_b = sb("xt_b", [DB + 1, TOK])
        ft_a = sb("ft_a", [P, TOK])
        ft_b = sb("ft_b", [FB + 1, TOK])
        h = sb("h", [P, NT, D])
        halves = sb("halves", [P, 2, 2 * H, 4, HS], fp32r)
        qk_t = sb("qk_t", [P, 2 * PAIRS, TOK], fp32r)
        v_aug = sb("v_aug", [P, NT, H, 2 * HS])
        neg_max = sb("neg_max", [P, 2, TPB, HG])
        max_parts = sb("max_parts", [P, 2, TPB, 2, HG], bf16)
        max_t = sb("max_t", [2 * HG, 2, S], bf16)
        probs = sb("probs", [P, 2, HG * (S + P)])
        recip = sb("recip", [P, 2, S])
        ctx_t = sb("ctx_t", [P, B, NG, S])
        best = sb("best", [P, NT])
        tie = sb("tie", [P, NT, NE])
        onehot = sb("onehot", [P, NT, NE])
        onehot_t = sb("onehot_t", [NE, TOK])
        others_t = sb("others_t", [NE, TOK], bf16)
        hidden = sb("hidden", [P, B, HC, S])
        skip = sb("skip", [P, NT, D])
        result = sb("result", [P, NT, D])

        big = [ctx.enter_context(nc.psum_tensor(f"big{i}", [P, 3 * 512], fp32)) for i in range(2)]
        small = [ctx.enter_context(nc.psum_tensor(f"small{i}", [P, 512], fp32)) for i in range(2)]

        ORDER = []
        for b in range(B):
            ORDER += [("tok_t", t) for t in (TPB * b, TPB * b + 1)]
            ORDER += [("tok", t) for t in (TPB * b, TPB * b + 1)]
        ORDER += [(stage, int(n)) for stage, n in (use.split() for use in (
            "x2_t 0, x2_t 1, qkv 0, qkv 1, turn 0, x2_t 2, x2_t 3, turn 1,"
            "scores 0, scores 1, max_t 0, qkv 2, expo 0, qkv 3, max_t 1, scores 2, turn 2, turn 3, pv 0, expo 1,"
            "max_t 2, scores 3, pv 1, expo 2, scores 4, max_t 3, pv 2, expo 3, scores 5, max_t 4, pv 3, expo 4,"
            "proj 0, proj 1, max_t 5, expo 5, pv 4, x3_t 0, x3_t 1, route 0, pv 5, hidden 0, onehot_t 0, mask 0,"
            "proj 2, proj 3, y 0, y 1, x3_t 2, x3_t 3, route 1, hidden 1, onehot_t 1, mask 1, y 2, y 3").split(","))]
        BIG = [use for use in ORDER if use[0] in ("qkv", "turn", "scores", "expo", "hidden")]
        SMALL = [[use for use in ORDER if use not in BIG and use[0] != "mask" and
                  (use[0] == "pv" if use[0] in ("pv", "max_t") else use[1] % 2) == w] for w in range(2)]

        def big_use(what):
            n = BIG.index(what)
            return n % 2, n // 2

        def small_use(what):
            w = 0 if what in SMALL[0] else 1
            return w, SMALL[w].index(what)

        img_in, up_in, zero_in = sem("img_in"), sem("up_in"), sem("zero_in")
        first_in = sem("first_in")
        pad_done = sem("pad_done")
        patches_done = sem("patches_done")
        tokens_in = [sem(f"tokens_in{t}") for t in range(NT)]
        tokw_in, qkvw_in, projw_in, rw_in = sem("tokw_in"), sem("qkvw_in"), sem("projw_in"), sem("rw_in")
        w1_in, w2_in = sem("w1_in"), sem("w2_in")
        gb_in = sem("gb_in")
        consts = sem("consts")
        idents = sem("idents")
        ones_set = sem("ones_set")
        stats_done = sem("stats_done")
        dve_step = sem("dve_step")
        pool_step = sem("pool_step")
        var_done = sem("var_done")
        rstd_done = sem("rstd_done")
        xn_done = sem("xn_done")
        ft_done, x2t_done, x3t_done = sem("ft_done"), sem("x2t_done"), sem("x3t_done")
        hi_done, lo_done = sem("hi_done"), sem("lo_done")
        turned, turned_rest = sem("turned"), sem("turned_rest")
        max_split = sem("max_split")
        maxt_done = sem("maxt_done")
        exp_done = sem("exp_done")
        causal_done = sem("causal_done")
        pv_out = sem("pv_out")
        qk_full = sem("qk_full")
        hidden_full = sem("hidden_full")
        even_scores, even_shifted = sem("even_scores"), sem("even_shifted")
        onehot_done, onehott_done = sem("onehot_done"), sem("onehott_done")
        hidden_done = sem("hidden_done")
        skip_done = sem("skip_done")
        result_done = sem("result_done")
        out_done = sem("out_done")
        big_full = [sem(f"big_full{i}") for i in range(2)]
        small_full = [sem(f"small_full{i}") for i in range(2)]
        h_in, h_out, logit_in, max_done = sem("h_in"), sem("h_out"), sem("logit_in"), sem("max_done")
        warm_set, recip_done, proj_zero = sem("warm_set"), sem("recip_done"), sem("proj_zero")

        block = ctx.enter_context(nc.Block())

        def cols(t):
            return slice(P * t, P * t + P)

        def regroup(queue, t):
            i0 = B * (G // TPB) * (t % TPB) + t // TPB
            queue.dma_start(tokens[:, t, :],
                            patches[i0:i0 + B * (G // TPB) - 1:B, :, :]).then_inc(tokens_in[t], 16)

        @block.sync
        def _(sp):
            x_rows = x.rearrange("b c (i r) w -> b i c (r w)", r=PATCH)
            for b in range(B):
                sp.dma_start(img[b:B * G:B, :, :].rearrange("i (c r) w -> i c (r w)", c=C),
                             x_rows[b]).then_inc(img_in, 16)
            sp.dma_start(first_up[:, :, SHIFT:PATCH, :], x[:, :, 0:SHIFT, :]).then_inc(first_in, 16)
            planes = tok_w.rearrange("(q c) n -> c q n", c=F // 16)
            sp.dma_start(tokw_a[:], planes[0:P // 16]).then_inc(tokw_in, 16)
            sp.dma_start(tokw_b[0:FB, :], planes[P // 16:]).then_inc(tokw_in, 16)
            sp.wait_ge(patches_done, 4)
            for t in (0, 2):
                regroup(sp, t)
            sp.dma_start(tokw_b[FB:FB + 1, :], tok_b.rearrange("(a n) -> a n", a=1)).then_inc(tokw_in, 16)
            sp.dma_start(qkvw_a[:], w_attn[0:P, :]).then_inc(qkvw_in, 16)
            sp.dma_start(qkvw_b[0:DB, :], w_attn[P:D, :]).then_inc(qkvw_in, 16)
            sp.dma_start(qkvw_b[DB:DB + 1, :], b_attn.rearrange("(a n) -> a n", a=1)).then_inc(qkvw_in, 16)
            sp.wait_ge(proj_zero, 1)
            heads = w_proj.rearrange("(g j d) n -> j d g n", g=NG, j=HG)
            for j in range(HG):
                sp.dma_start(projw[2 * HS * j:2 * HS * j + HS, :, :], heads[j]).then_inc(projw_in, 16)
            sp.dma_start(projw[HS:HS + 1, 0, :], b_proj.rearrange("(a n) -> a n", a=1)).then_inc(projw_in, 16)
            sp.dma_start(rw_a[:], router_w[0:P, :]).then_inc(rw_in, 16)
            sp.dma_start(rw_b[0:DB, :], router_w[P:D, :]).then_inc(rw_in, 16)
            sp.dma_start(rw_b[DB:DB + 1, :], router_b.rearrange("(a n) -> a n", a=1)).then_inc(rw_in, 16)
            w1_v = w1.rearrange("e d n -> d e n")
            sp.dma_start(w1_a[:].rearrange("d (e n) -> d e n", e=NE), w1_v[0:P]).then_inc(w1_in, 16)
            sp.dma_start(w1_b[0:DB, :].rearrange("d (e n) -> d e n", e=NE), w1_v[P:D]).then_inc(w1_in, 16)
            sp.dma_start(w1_b[DB:DB + 1, :], b1.rearrange("e (a n) -> a (e n)", a=1)).then_inc(w1_in, 16)
            sp.dma_start(w2_sb[:], w2.rearrange("e n d -> (e n) d").rearrange("(c p) d -> p c d", p=P))\
                .then_inc(w2_in, 16)
            sp.dma_start(b2_sb[:], b2).then_inc(w2_in, 16)
            for t in range(NT):
                sp.wait_ge(result_done, t + 1)
                sp.dma_start(out[t // TPB, cols(t % TPB), :], result[:, t, :]).then_inc(out_done, 16)
            sp.wait_ge(out_done, 16 * NT)

        @block.gpsimd
        def _(pool):
            step = [0]

            def link(ins):
                step[0] += 1
                ins.then_inc(pool_step, 1)
                pool.wait_ge(pool_step, step[0])

            link(nc.gpsimd.memset(ident[:], 0.0))
            link(nc.gpsimd.affine_select(out=ident[:], in_=ident[:], compare_op=ALU.not_equal, fill=1.0,
                                         base=0, pattern=[[-1, P]], channel_multiplier=1))
            nc.gpsimd.tensor_copy(ident_b[:], ident[:]).then_inc(idents, 1)
            link(nc.gpsimd.memset(minus_half[:], -0.5))
            link(nc.gpsimd.memset(later[:], 0.0))
            nc.gpsimd.affine_select(out=later[:], in_=later[:], compare_op=ALU.is_ge, fill=MASKED,
                                    base=0, pattern=[[-1, P]], channel_multiplier=1).then_inc(consts, 1)
            nc.gpsimd.memset(ones[:], 1.0).then_inc(consts, 1)
            nc.gpsimd.memset(projw[:], 0.0).then_inc(proj_zero, 1)
            link(nc.gpsimd.memset(head_rows[:], 0.0))
            link(nc.gpsimd.affine_select(out=head_rows[:], in_=head_rows[:], compare_op=ALU.not_equal,
                                         fill=1.0, base=0, pattern=[[-1, HG], [0, P]], channel_multiplier=1))
            nc.gpsimd.affine_select(out=head_rows[:], in_=head_rows[:], compare_op=ALU.not_equal,
                                    fill=1.0, base=-HG, pattern=[[-1, HG], [0, P]],
                                    channel_multiplier=1).then_inc(consts, 1)
            pool.wait_ge(patches_done, 4)
            regroup(pool, 3)
            link(nc.gpsimd.memset(expert_rows[:], 0.0))
            ev = expert_rows[:].rearrange("e (f n) -> e f n", f=NE)
            nc.gpsimd.affine_select(out=ev, in_=ev, compare_op=ALU.not_equal, fill=OFF, base=0,
                                    pattern=[[-1, NE], [0, HID]], channel_multiplier=1).then_inc(consts, 1)
            for e in range(NE):
                link(nc.gpsimd.memset(first_wins[:, :, e:e + 1], float(NE - e)))
            n_rstd = [0]

            def rstds(b):
                n_rstd[0] += 1
                pool.wait_ge(var_done, n_rstd[0])
                s = slice(TPB * b, TPB * b + TPB)
                nc.gpsimd.tensor_tensor(rstd[:, s], var_eps[:, s], minus_half[:], ALU.pow).then_inc(rstd_done, 1)

            def causal(u):
                pool.wait_ge(exp_done, u + 1)
                on = probs[:, u % 2, 0:HG * S].rearrange("p (g q) -> p g q", g=HG)[:, :, 0:P]
                off = probs[:, u % 2, HG * S:].rearrange("p (g q) -> p g q", g=HG)
                for blk in (on, off):
                    nc.gpsimd.affine_select(out=blk, in_=blk, compare_op=ALU.is_ge, fill=0.0, base=0,
                                            pattern=[[0, HG], [1, P]], channel_multiplier=-1)\
                        .then_inc(causal_done, 1)

            def skips(b):
                pool.wait_ge(xn_done, 2 * NT + TPB * b + TPB)
                s = slice(TPB * b, TPB * b + TPB)
                nc.gpsimd.tensor_tensor(skip[:, s, :], h[:, s, :], xn[:, s, 0:D], ALU.add)\
                    .then_inc(skip_done, 1)

            rstds(0)
            rstds(1)
            for stage, n in ORDER:
                if stage == "expo":
                    causal(n)
                if stage in ("tok", "proj") and n % TPB == TPB - 1:
                    rstds(n // TPB)
                if stage == "proj" and n % TPB == TPB - 1:
                    skips(n // TPB)

        @block.scalar
        def _(act):
            def affine_in(n, vec):
                planes = vec.rearrange("(q c a) -> c q a", c=F // 16, a=1)
                with nc.allow_non_contiguous_dma(reason="a small vector"):
                    act.dma_start(gb_a[:, n:n + 1], planes[0:P // 16]).then_inc(gb_in, 16)
                    act.dma_start(gb_b[0:FB, n:n + 1], planes[P // 16:]).then_inc(gb_in, 16)

            for b in range(B):
                rows = x[b, :, SHIFT:IMG - SHIFT, :].rearrange("c (i r) w -> i c (r w)", r=PATCH)
                act.dma_start(img_up[B + b:B * G:B, :, :].rearrange("i (c r) w -> i c (r w)", c=C),
                              rows).then_inc(up_in, 16)
            affine_in(0, tok_gamma)
            act.wait_ge(patches_done, 4)
            regroup(act, 1)
            affine_in(1, tok_beta)
            act.wait_ge(warm_set, 1)
            nc.scalar.activation(first_act[:], warm[:, 0:1], ACT.Identity)

            def small_in(what):
                w, n = small_use(what)
                act.wait_ge(small_full[w], n + 1)
                return w

            def tok_turned(t):
                w = small_in(("tok_t", t))
                nc.scalar.activation(ft_a[:, cols(t)], small[w][:, 0:P], ACT.Identity, bias=gb_a[:, 1:2],
                                     scale=gb_a[:, 0:1]).then_inc(ft_done, 1)
                nc.scalar.activation(ft_b[0:FB, cols(t)], small[w][0:FB, P:2 * P], ACT.Identity,
                                     bias=gb_b[:, 1:2], scale=gb_b[:, 0:1]).then_inc(ft_done, 1)

            def turned_copy(what, dst_a, dst_b, done):
                w = small_in(what)
                t = what[1]
                nc.scalar.activation(dst_a[:, cols(t)], small[w][:, 0:P], ACT.Copy).then_inc(done, 1)
                nc.scalar.activation(dst_b[0:DB, cols(t)], small[w][0:DB, P:2 * P], ACT.Copy).then_inc(done, 1)

            def split_high(t):
                a, n = big_use(("qkv", t))
                act.wait_ge(qk_full, t + 1)
                if t >= 2:
                    a2, n2 = big_use(("turn", t - 2))
                    act.wait_ge(big_full[a2], n2 + 1)
                q = big[a][:, 0:D].rearrange("p (n d) -> p n d", n=H)
                k = big[a][:, D:2 * D].rearrange("p (n d) -> p n d", n=H)
                nc.scalar.activation(halves[:, t % 2, 0:H, 0:2, :], q.unsqueeze(2).to_broadcast([P, H, 2, HS]),
                                     ACT.Copy).then_inc(hi_done, 1)
                nc.scalar.activation(halves[:, t % 2, H:2 * H, 0:4:2, :],
                                     k.unsqueeze(2).to_broadcast([P, H, 2, HS]), ACT.Copy).then_inc(hi_done, 1)
                act.wait_ge(big_full[a], n + 1)
                v = big[a][:, 512:512 + D].rearrange("p (n d) -> p n d", n=H)
                nc.scalar.activation(v_aug[:, t, :, 0:HS], v, ACT.Copy).then_inc(hi_done, 1)

            def turned_halves(t):
                a, n = big_use(("turn", t))
                act.wait_ge(big_full[a], n + 1)
                nc.scalar.activation(qk_t[:, 0:8, cols(t)],
                                     big[a][:, 0:2 * 512].rearrange("p (n q) -> p n q", n=8),
                                     ACT.Copy).then_inc(turned, 1)

            def max_rows(u):
                w = small_in(("max_t", u))
                if u >= 2:
                    a, n = big_use(("expo", u - 2))
                    act.wait_ge(big_full[a], n + 1)
                src = small[w][0:2 * HG, 0:P].bitcast(bf16)
                nc.scalar.activation(max_t[:, u % 2, :], src, ACT.Copy).then_inc(maxt_done, 1)

            def exps(u):
                a, n = big_use(("expo", u))
                act.wait_ge(big_full[a], n + 1)
                if u >= 2:
                    w, m = small_use(("pv", u - 2))
                    act.wait_ge(small_full[w], m + 1)
                nc.scalar.activation(probs[:, u % 2, :], big[a][:, :], ACT.Exp, scale=SCALE).then_inc(exp_done, 1)

            def gelu(b):
                a, _ = big_use(("hidden", b))
                for c in range(0, HC, 2):
                    act.wait_ge(hidden_full, (HC * b + c) // 2 + 1)
                    nc.scalar.activation(hidden[:, b, c:c + 2, :],
                                         big[a][:, S * c:S * (c + 2)].rearrange("p (c q) -> p c q", c=2),
                                         ACT.Gelu).then_inc(hidden_done, 1)

            act.wait_ge(gb_in, 16 * 4)
            act.wait_ge(ones_set, 2)
            for stage, n in ORDER:
                if stage == "tok_t":
                    tok_turned(n)
                if stage == "x2_t":
                    turned_copy(("x2_t", n), xt_a, xt_b, x2t_done)
                if stage == "qkv":
                    split_high(n)
                if stage == "turn":
                    turned_halves(n)
                if stage == "max_t":
                    max_rows(n)
                if stage == "expo":
                    exps(n)
                if stage == "x3_t":
                    turned_copy(("x3_t", n), xt_a, xt_b, x3t_done)
                if stage == "mask":
                    gelu(n)

        @block.vector
        def _(dve):
            step = [0]

            def link(ins):
                step[0] += 1
                ins.then_inc(dve_step, 1)
                dve.wait_ge(dve_step, step[0])

            def small_in(what):
                w, n = small_use(what)
                dve.wait_ge(small_full[w], n + 1)
                return w

            def big_in(what):
                a, n = big_use(what)
                dve.wait_ge(big_full[a], n + 1)
                return a

            nc.vector.memset(warm[:], 0.0).then_inc(warm_set, 1)
            nc.vector.memset(first_up[:, :, 0:SHIFT, :], 0.0).then_inc(zero_in, 1)
            nc.vector.memset(patches[:, 0, 2 * FK:3 * FK], 0.0).then_inc(pad_done, 1)
            nc.vector.memset(ft_b[:], 1.0).then_inc(ones_set, 1)
            dve.wait_ge(idents, 1)
            nc.vector.tensor_copy(ident_r[:], ident[:]).then_inc(idents, 1)

            def patch_view(k, j0=0):
                return patches[:, j0:G, FK * k:FK * k + FK].rearrange("p j (r c) -> p j r c", c=PATCH)

            dve.wait_ge(img_in, 16 * B)
            nc.vector.tensor_copy(patch_view(0), img[:].rearrange("p r (j c) -> p j r c", c=PATCH))\
                .then_inc(patches_done, 1)
            nc.vector.tensor_copy(
                patch_view(2, 1),
                img[:, :, SHIFT:IMG - SHIFT].rearrange("p r (j c) -> p j r c", c=PATCH)).then_inc(patches_done, 1)
            dve.wait_ge(pad_done, 1)
            nc.vector.tensor_copy(patch_view(2)[:, 0, :, SHIFT:PATCH], img[:, :, 0:SHIFT]).then_inc(patches_done, 1)
            dve.wait_ge(up_in, 16 * B)
            dve.wait_ge(first_in, 16)
            dve.wait_ge(zero_in, 1)
            nc.vector.tensor_copy(patch_view(1), img_up[:].rearrange("p r (j c) -> p j r c", c=PATCH))\
                .then_inc(patches_done, 1)

            n_rstd = [0]

            stats_of = [0]

            def normalise(src, b, eps, width):
                ts = range(TPB * b, TPB * b + TPB)
                stats_of[0] += TPB
                dve.wait_ge(stats_done, stats_of[0])
                for t in ts:
                    last = nc.vector.bn_aggr(mv[:, t, :], stats[:, t, :])
                    last.then_inc(dve_step, 1)
                    step[0] += 1
                dve.wait_ge(dve_step, step[0])
                nc.vector.tensor_scalar(var_eps[:, ts[0]:ts[-1] + 1], mv[:, ts[0]:ts[-1] + 1, 1], eps, None,
                                        ALU.add).then_inc(var_done, 1)
                n_rstd[0] += 1
                dve.wait_ge(rstd_done, n_rstd[0])
                if width == D and n_rstd[0] <= 2 * B:
                    dve.wait_ge(h_in, TPB * b + TPB)
                for t in ts:
                    nc.vector.tensor_scalar(xn[:, t, 0:width], src(t), mv[:, t, 0:1], rstd[:, t:t + 1],
                                            ALU.subtract, ALU.mult).then_inc(xn_done, 1)

            def split_low(t):
                a, _ = big_use(("qkv", t))
                dve.wait_ge(hi_done, 3 * t + 2)
                q = big[a][:, 0:D].rearrange("p (n d) -> p n d", n=H)
                k = big[a][:, D:2 * D].rearrange("p (n d) -> p n d", n=H)
                wide = [P, H, 2, HS]
                for x_, rows, slots in ((q, slice(0, H), slice(2, 4)), (k, slice(H, 2 * H), slice(1, 4, 2))):
                    nc.vector.tensor_tensor(
                        halves[:, t % 2, rows, slots, :], x_.unsqueeze(2).to_broadcast(wide),
                        halves[:, t % 2, rows, 0, :].bitcast(fp32).unsqueeze(2).to_broadcast(wide),
                        ALU.subtract).then_inc(lo_done, 1)

            def turned_halves(t):
                a = big_in(("turn", t))
                nc.vector.tensor_copy(qk_t[:, 8:2 * PAIRS, cols(t)],
                                      big[a][:, 2 * 512:3 * 512].rearrange("p (n q) -> p n q", n=4))\
                    .then_inc(turned_rest, 1)

            def maxima(u):
                a = big_in(("scores", u))
                if u >= 2:
                    w, n = small_use(("max_t", u - 2))
                    dve.wait_ge(small_full[w], n + 1)
                p = u % 2
                nc.vector.tensor_reduce(neg_max[:, p, 0, :],
                                        big[a][:, 2 * 512:3 * 512].rearrange("p (g k) -> p g k", g=HG),
                                        AX.X, ALU.max, negate=True).then_inc(max_done, 1)
                nc.vector.tensor_reduce(neg_max[:, p, 1, :],
                                        big[a][:, 0:2 * 512].rearrange("p (g k) -> p g k", g=HG),
                                        AX.X, ALU.max, negate=True).then_inc(max_done, 1)
                dve.wait_ge(max_done, 2 * u + 2)
                link(nc.vector.tensor_copy(max_parts[:, p, :, 0, :], neg_max[:, p, :, :]))
                nc.vector.tensor_tensor(max_parts[:, p, :, 1, :], neg_max[:, p, :, :],
                                        max_parts[:, p, :, 0, :], ALU.subtract).then_inc(max_split, 1)

            def context(u):
                w = small_in(("pv", u))
                nc.vector.reciprocal(recip[:, u % 2, :], small[w][:, S:2 * S]).then_inc(recip_done, 1)
                dve.wait_ge(recip_done, u + 1)
                nc.vector.tensor_tensor(ctx_t[:, u // NG, u % NG, :], small[w][:, 0:S], recip[:, u % 2, :],
                                        ALU.mult).then_inc(pv_out, 1)

            def attention_out(t):
                w = small_in(("proj", t))
                nc.vector.tensor_tensor(h[:, t, :], small[w][:, 0:D], h[:, t, :], ALU.add).then_inc(h_out, 1)
                dve.wait_ge(h_out, t + 1)
                nc.vector.bn_stats(stats[:, t, :], h[:, t, :]).then_inc(stats_done, 1)

            def route(b):
                w = small_in(("route", b))
                s = slice(TPB * b, TPB * b + TPB)
                logit = small[w][:, 0:TPB * NE].rearrange("p (t e) -> p t e", t=TPB)
                top = best[:, s].unsqueeze(2).to_broadcast([P, TPB, NE])
                link(nc.vector.tensor_reduce(best[:, s], logit, AX.X, ALU.max))
                nc.vector.tensor_tensor(tie[:, s, :], logit, top, ALU.is_equal).then_inc(logit_in, 1)
                dve.wait_ge(logit_in, b + 1)
                link(nc.vector.tensor_tensor(tie[:, s, :], tie[:, s, :], first_wins[:], ALU.mult))
                link(nc.vector.tensor_reduce(best[:, s], tie[:, s, :], AX.X, ALU.max))
                nc.vector.tensor_tensor(onehot[:, s, :], tie[:, s, :], top, ALU.is_equal)\
                    .then_inc(onehot_done, 1)

            def onehot_rows(b):
                w = small_in(("onehot_t", b))
                s = slice(S * b, S * b + S)
                nc.vector.tensor_scalar(others_t[:, s], small[w][0:NE, 0:S], 1.0, None,
                                        ALU.subtract).then_inc(onehott_done, 1)
                nc.vector.tensor_copy(onehot_t[:, s], small[w][0:NE, 0:S]).then_inc(onehott_done, 1)

            def last_sum(t):
                w = small_in(("y", t))
                dve.wait_ge(skip_done, t // TPB + 1)
                nc.vector.tensor_tensor(result[:, t, :], small[w][:, 0:D], skip[:, t, :],
                                        ALU.add).then_inc(result_done, 1)

            nc.vector.memset(xt_b[DB:DB + 1, :], 1.0).then_inc(ones_set, 1)
            nc.vector.memset(v_aug[:, :, :, HS:2 * HS], 1.0).then_inc(ones_set, 1)

            for b in range(B):
                for t in (TPB * b, TPB * b + 1):
                    dve.wait_ge(tokens_in[t], 16)
                    nc.vector.bn_stats(stats[:, t, :], tokens[:, t, :]).then_inc(stats_done, 1)
                normalise(lambda t: tokens[:, t, :], b, TOK_EPS, F)
            for stage, n in ORDER:
                if stage == "tok":
                    w = small_in(("tok", n))
                    nc.vector.bn_stats(stats[:, n, :], small[w][:, 0:D]).then_inc(stats_done, 1)
                    nc.vector.tensor_copy(h[:, n, :], small[w][:, 0:D]).then_inc(h_in, 1)
                if stage == "proj":
                    attention_out(n)
                if stage in ("tok", "proj") and n % TPB == TPB - 1:
                    normalise(lambda t: h[:, t, :], n // TPB, EPS, D)
                if stage == "qkv":
                    split_low(n)
                if stage == "turn":
                    turned_halves(n)
                if stage == "scores":
                    maxima(n)
                if stage == "pv":
                    context(n)
                if stage == "route":
                    route(n)
                if stage == "onehot_t":
                    onehot_rows(n)
                if stage == "y":
                    last_sum(n)

        @block.tensor
        def _(pe):
            def read_by(what):
                stage, n = what
                return {
                    "tok_t": (ft_done, 2 * n + 2), "tok": (h_in, n + 1), "x2_t": (x2t_done, 2 * n + 2),
                    "qkv": (lo_done, 2 * n + 2), "turn": (turned, n + 1),
                    "scores": (max_done, 2 * n + 2), "max_t": (maxt_done, n + 1),
                    "expo": (exp_done, n + 1), "pv": (pv_out, n + 1),
                    "proj": (h_out, n + 1),
                    "x3_t": (x3t_done, 2 * n + 2), "route": (logit_in, n + 1),
                    "onehot_t": (onehott_done, 2 * n + 2), "hidden": (hidden_done, HC // 2 * (n + 1)),
                    "y": (result_done, n + 1),
                }[stage]

            def ready(what):
                w, n = small_use(what)
                if n:
                    pe.wait_ge(*read_by(SMALL[w][n - 1]))
                return w

            def big_ready(what):
                a, n = big_use(what)
                if n:
                    last = BIG[2 * (n - 1) + a]
                    pe.wait_ge(*read_by(last))
                    if last[0] == "qkv":
                        pe.wait_ge(hi_done, 3 * last[1] + 3)
                    if last[0] == "turn":
                        pe.wait_ge(turned_rest, last[1] + 1)
                return a

            def mm(o, l, r, start=True, stop=True, **k):
                return nc.tensor.matmul(o, l, r, start=start, stop=stop, **k)

            def turn(what, src, width):
                w = ready(what)
                nc.tensor.transpose(small[w][:, 0:P], src[:, 0:P], ident[:])
                nc.tensor.transpose(small[w][0:width - P, P:2 * P], src[:, P:width], ident[:])\
                    .then_inc(small_full[w], 1)

            def rows_out(what, xa, xb, wa, wb, width):
                w = ready(what)
                t = what[1]
                mm(small[w][:, 0:width], xa[:, cols(t)], wa, stop=False)
                mm(small[w][:, 0:width], xb[:, cols(t)], wb, start=False).then_inc(small_full[w], 1)

            def qkv(t):
                a = big_ready(("qkv", t))
                pe.wait_ge(x2t_done, 2 * t + 2)
                for o, c0, c1 in ((0, 0, 2 * D), (512, 2 * D, 3 * D)):
                    mm(big[a][:, o:o + c1 - c0], xt_a[:, cols(t)], qkvw_a[:, c0:c1], stop=False)
                    last = mm(big[a][:, o:o + c1 - c0], xt_b[:, cols(t)], qkvw_b[:, c0:c1], start=False)
                    if o == 0:
                        last.then_inc(qk_full, 1)
                last.then_inc(big_full[a], 1)

            def turn_halves(t):
                a = big_ready(("turn", t))
                pe.wait_ge(lo_done, 2 * t + 2)
                pe.wait_ge(hi_done, 3 * t + 3)
                for n in range(2 * PAIRS):
                    last = nc.tensor.transpose(
                        big[a][:, P * n:P * n + P].bitcast(fp32r),
                        halves[:, t % 2, 2 * n:2 * n + 2, :, :].rearrange("p n s d -> p (n s d)"), ident_r[:])
                last.then_inc(big_full[a], 1)

            def qk(hd, which, b, c0, c1):
                r = SLOT * (hd % 2)
                return qk_t[r:r + SLOT, PAIRS * which + hd // 2, S * b + c0:S * b + c1]

            def scores(u):
                a = big_ready(("scores", u))
                b, g = u // NG, u % NG
                areas = [(big[a][:, 0:512].rearrange("p (g k) -> p g k", g=2), S, P),
                         (big[a][:, 512:1024].rearrange("p (g k) -> p g k", g=2), S, P),
                         (big[a][:, 1024:1536].rearrange("p (g k) -> p g k", g=HG), P, 0)]
                for area, width, q0 in areas:
                    mm(area[:, :, width - P:width], ident_b[:],
                       later[:].unsqueeze(1).to_broadcast([P, 512 // width, P]), skip_group_check=True)
                for n, k0, odd in ((2, 0, 0), (0, 0, 0), (1, 0, 1), (2, 2, 1)):
                    area, width, q0 = areas[n]
                    if (n, odd) == (2, 1):
                        pe.wait_ge(even_scores, u + 1)
                    for j in range(2):
                        hd = HG * g + 2 * j + odd
                        last = mm(area[:, k0 + j, :], qk(hd, 0, b, q0, q0 + P), qk(hd, 1, b, 0, width),
                                  start=False, skip_group_check=True)
                    if (n, odd) == (2, 0):
                        last.then_inc(even_scores, 1)
                last.then_inc(big_full[a], 1)

            def max_rows(u):
                w = ready(("max_t", u))
                pe.wait_ge(max_split, u + 1)
                for i in range(TPB):
                    last = nc.tensor.transpose(
                        small[w][0:2 * HG, 64 * i:64 * i + 64].bitcast(bf16),
                        max_parts[:, u % 2, i, :, :].rearrange("p s g -> p (s g)"), ident_b[:])
                last.then_inc(small_full[w], 1)

            def shifted_scores(u):
                a = big_ready(("expo", u))
                b, g = u // NG, u % NG
                pe.wait_ge(maxt_done, u + 1)

                def place(j, k0):
                    c = (512 * (j % 2) + S * (j // 2)) if k0 == 0 else 1024 + P * (2 * (j % 2) + j // 2)
                    return big[a][:, c:c + S - k0]

                for k0 in (0, P):
                    for j in (0, 2, 1, 3):
                        first = j < 2 if k0 == 0 else j == 0
                        mm(place(j, k0), head_rows[:, 2 * (j % 2) + j // 2, :], max_t[:, u % 2, k0:S], start=first,
                           skip_group_check=True)
                for k0, js in ((P, (0, 2)), (0, (0, 2)), (0, (1, 3)), (P, (1, 3))):
                    if (k0, js[0]) == (P, 1):
                        pe.wait_ge(even_shifted, u + 1)
                    for j in js:
                        hd = HG * g + j
                        last = mm(place(j, k0), qk(hd, 1, b, k0, k0 + P), qk(hd, 0, b, k0, S),
                                  start=False, skip_group_check=True)
                    if (k0, js[0]) == (P, 0):
                        last.then_inc(even_shifted, 1)
                last.then_inc(big_full[a], 1)

            def values(u):
                w = ready(("pv", u))
                b, g = u // NG, u % NG
                for of_ones in (0, 1):
                    for k, (o, q0) in enumerate(((0, 0), (HG * S, P))):
                        if not of_ones:
                            pe.wait_ge(causal_done, 2 * u + k + 1)
                        for j in range(HG):
                            n = 2 * (j % 2) + j // 2
                            pr = probs[:, u % 2, o + (S - q0) * n:o + (S - q0) * (n + 1)]
                            v = ones[:] if of_ones else v_aug[:, TPB * b + k, HG * g + j, :]
                            last = mm(small[w][32 * j:32 * j + 32, S * of_ones + q0:S * of_ones + S], v, pr,
                                      start=(k == 0), stop=(k == 1), skip_group_check=True)
                last.then_inc(small_full[w], 1)

            def project(t):
                w = ready(("proj", t))
                b = t // TPB
                pe.wait_ge(pv_out, NG * (b + 1))
                for g in range(NG):
                    last = mm(small[w][:, 0:D], ctx_t[:, b, g, cols(t % TPB)], projw[:, g, :], start=(g == 0),
                              stop=(g == NG - 1))
                last.then_inc(small_full[w], 1)

            def hidden_in(b):
                a = big_ready(("hidden", b))
                pe.wait_ge(x3t_done, 2 * TPB * (b + 1))
                s = slice(S * b, S * b + S)
                for c in range(HC):
                    o = big[a][:, S * c:S * c + S]
                    mm(o, w1_a[:, P * c:P * c + P], xt_a[:, s], start=(c % 2 == 0), skip_group_check=True)
                    mm(o, w1_b[:, P * c:P * c + P], xt_b[:, s], start=False, skip_group_check=True)

            def mask_experts(b):
                a, _ = big_use(("hidden", b))
                pe.wait_ge(onehott_done, 2 * b + 1)
                s = slice(S * b, S * b + S)
                for c in range(HC):
                    last = mm(big[a][:, S * c:S * c + S], expert_rows[:, P * c:P * c + P], others_t[:, s],
                              start=False, skip_group_check=True)
                    if c % 2:
                        last.then_inc(hidden_full, 1)

            def experts_out(t):
                w = ready(("y", t))
                b = t // TPB
                pe.wait_ge(onehott_done, 2 * b + 2)
                mm(small[w][:, 0:D], onehot_t[:, cols(t)], b2_sb[:], stop=False)
                for c in range(HC):
                    if c % 2 == 0:
                        pe.wait_ge(hidden_done, (HC * b + c) // 2 + 1)
                    last = mm(small[w][:, 0:D], hidden[:, b, c, cols(t % TPB)], w2_sb[:, c, :],
                              start=False, stop=(c == HC - 1))
                last.then_inc(small_full[w], 1)

            def keep_warm(n):
                for i in range(n):
                    mm(big[1][:, 0:512], warm[:, 0:P], warm[:])

            pe.wait_ge(warm_set, 1)
            keep_warm(START[0])
            pe.wait_ge(idents, 2)
            pe.wait_ge(ones_set, 2)
            for stage, n in ORDER:
                if (stage, n) in STEADY:
                    use, count = STEADY[stage, n]
                    w = ready(use)
                    for i in range(count):
                        mm(small[w][:, :], warm[:, 0:P], warm[:])
                if stage == "tok_t":
                    pe.wait_ge(xn_done, n + 1)
                    turn(("tok_t", n), xn[:, n, :], F)
                    keep_warm(FILL["tok_t"][n])
                if stage == "tok":
                    pe.wait_ge(tokw_in, 16 * 3)
                    pe.wait_ge(ft_done, 2 * n + 2)
                    rows_out(("tok", n), ft_a, ft_b, tokw_a[:], tokw_b[:], D)
                    keep_warm(FILL["tok"][n])
                if stage == "x2_t":
                    pe.wait_ge(xn_done, NT + n + 1)
                    turn(("x2_t", n), xn[:, n, :], D)
                    if n < TPB:
                        keep_warm(FILL["x2_t"][n])
                if stage == "qkv":
                    pe.wait_ge(qkvw_in, 16 * 3)
                    qkv(n)
                if stage == "turn":
                    turn_halves(n)
                if stage == "scores":
                    pe.wait_ge(consts, 4)
                    pe.wait_ge(ones_set, 3)
                    pe.wait_ge(turned, TPB * (n // NG + 1))
                    pe.wait_ge(turned_rest, TPB * (n // NG + 1))
                    scores(n)
                if stage == "max_t":
                    max_rows(n)
                if stage == "expo":
                    shifted_scores(n)
                if stage == "pv":
                    values(n)
                if stage == "proj":
                    pe.wait_ge(projw_in, 16 * (HG + 1))
                    project(n)
                if stage == "x3_t":
                    pe.wait_ge(xn_done, 2 * NT + n + 1)
                    turn(("x3_t", n), xn[:, n, :], D)
                if stage == "route":
                    pe.wait_ge(rw_in, 16 * 3)
                    w = ready(("route", n))
                    pe.wait_ge(x3t_done, 2 * TPB * (n + 1))
                    for i in range(TPB):
                        o, c = small[w][:, NE * i:NE * i + NE], cols(TPB * n + i)
                        mm(o, xt_a[:, c], rw_a[:], stop=False)
                        last = mm(o, xt_b[:, c], rw_b[:], start=False)
                    last.then_inc(small_full[w], 1)
                if stage == "onehot_t":
                    w = ready(("onehot_t", n))
                    pe.wait_ge(onehot_done, n + 1)
                    for i in range(TPB):
                        last = nc.tensor.transpose(small[w][0:NE, P * i:P * i + P], onehot[:, TPB * n + i, :],
                                                   ident[:])
                    last.then_inc(small_full[w], 1)
                if stage == "hidden":
                    pe.wait_ge(w1_in, 16 * 3)
                    hidden_in(n)
                if stage == "mask":
                    mask_experts(n)
                if stage == "y":
                    pe.wait_ge(w2_in, 16 * 2)
                    experts_out(n)


_INS = ['x', 'L0_tok_ln_gamma', 'L0_tok_ln_beta', 'L0_tok_W', 'L0_tok_b', 'L0_attn_W_attn', 'L0_attn_b_attn',
        'L0_attn_W_proj', 'L0_attn_b_proj', 'L0_ffn_router_w', 'L0_ffn_router_b', 'L0_ffn_w1', 'L0_ffn_b1',
        'L0_ffn_w2', 'L0_ffn_b2']


def kernel(**inputs):
    import numpy as _np
    import concourse.bacc as _bacc
    from concourse import mybir as _mybir
    from concourse.bass_utils import run_bass_kernel_spmd as _run

    nc = _bacc.Bacc("TRN2", target_bir_lowering=False, num_devices=1)
    arrays, args = {}, []
    for name in _INS:
        a = _np.ascontiguousarray(inputs[name])
        arrays[f"in_{name}_dram"] = a
        args.append(nc.dram_tensor(f"in_{name}_dram", a.shape, _mybir.dt.from_np(a.dtype), kind="ExternalInput").ap())
    out = nc.dram_tensor("out_dram", (2, 256, 192), _mybir.dt.float32, kind="ExternalOutput").ap()
    vit_tower(nc, *args, out)
    r = _run(nc, [arrays], core_ids=[0])
    return r.results[0]["out_dram"]
```

```python
import concourse.bass as bass
from concourse import mybir
from contextlib import ExitStack


def vit_tower(nc, x, tok_gamma, tok_beta, tok_w, tok_b, w_attn, b_attn, w_proj, b_proj,
              router_w, router_b, w1, b1, w2, b2, out):
    fp32 = mybir.dt.float32
    fp32r = mybir.dt.float32r
    bf16 = mybir.dt.bfloat16
    ALU = mybir.AluOpType
    ACT = mybir.ActivationFunctionType
    AX = mybir.AxisListType

    P = 128
    B, C, IMG, _ = x.shape
    PATCH = 4
    SHIFT = PATCH // 2
    G = IMG // PATCH
    ROWS = C * PATCH
    KINDS = 3
    FK = ROWS * PATCH
    F = KINDS * FK
    FB = F - P
    D = tok_w.shape[1]
    DB = D - P
    S = G * G
    TPB = S // P
    NT = B * TPB
    TOK = B * S
    H = 12
    HS = D // H
    HG = 4
    NG = H // HG
    UNITS = B * NG
    PAIRS = H // 2
    SLOT = 4 * HS
    NE, HID = router_w.shape[1], w1.shape[2]
    NH = NE * HID
    HC = NH // P
    TOK_EPS = 1e-5
    EPS = 1e-5
    SCALE = float(HS) ** -0.5
    MASKED = -1e30
    START = 36
    FILL = {("tok_t", 1): 2, ("tok", 1): 13, ("x2_t", 1): 2}
    STEADY = {("qkv", 3): (("pv", 0), 4)}
    BEFORE = {("qkv", 2): 3}
    OFF = float(2 ** 30)

    ctx = ExitStack()
    with ctx:
        def sb(name, shape, dt=fp32):
            return ctx.enter_context(nc.sbuf_tensor(name, shape, dt))

        def sem(name):
            return ctx.enter_context(nc.semaphore(name))

        img = sb("img", [B * G, ROWS, IMG])
        img_up = sb("img_up", [B * G, ROWS, IMG])
        first_up = img_up[0:B, :, :].rearrange("i (c r) w -> i c r w", c=C)
        patches = sb("patches", [B * G, G, F])
        tokens = sb("tokens", [P, NT, F])
        tokw_a = sb("tokw_a", [P, D])
        tokw_b = sb("tokw_b", [FB + 1, D])
        gb_a = sb("gb_a", [P, 2])
        gb_b = sb("gb_b", [FB, 2])
        qkvw = sb("qkvw", [P, 3, 3 * D])
        qkvw_hi = sb("qkvw_hi", [P, 3, 3 * D], fp32r)
        qkvw_lo = sb("qkvw_lo", [P, 2, 3 * D], fp32r)
        rw = sb("rw", [P, 3, NE])
        rw_hi = sb("rw_hi", [P, 3, NE], fp32r)
        rw_lo = sb("rw_lo", [P, 2, NE], fp32r)
        w1_sb = sb("w1_sb", [P, 3, NH])
        w1_hi = sb("w1_hi", [P, 3, NH], fp32r)
        w1_lo = sb("w1_lo", [P, 2, NH], fp32r)
        NB1, NB2 = 3 * D // DB, NH // DB
        bias_in = sb("bias_in", [DB, NB1 + NB2 + 1])
        bias_parts = sb("bias_parts", [DB, 2, NB1 + NB2 + 1], fp32r)
        qkv_bias = sb("qkv_bias", [2, 3 * D], fp32r)
        r_bias = sb("r_bias", [2, NE], fp32r)
        projw = sb("projw", [P, NG, TPB, D])
        projb = sb("projb", [P, D])
        w2_sb = sb("w2_sb", [P, HC, D])
        b2_sb = sb("b2_sb", [NE, D])
        b2_hi = sb("b2_hi", [NE, D], fp32r)
        b2_lo = sb("b2_lo", [NE, D], fp32r)
        ident = sb("ident", [P, P])
        ident_r = sb("ident_r", [P, P], fp32r)
        ident_b = sb("ident_b", [P, P], bf16)
        later = sb("later", [P, P], bf16)
        expert_rows = sb("expert_rows", [NE + 2, NH])
        hid_rows = sb("hid_rows", [NE + 2, NH], fp32r)
        ones_r = sb("ones_r", [2, P], fp32r)
        ones = sb("ones", [P, TPB + 1, HS])
        warm = sb("warm", [P, 512], bf16)
        first_act = sb("first_act", [P, 1])
        minus_half = sb("minus_half", [P, TPB])
        first_wins = sb("first_wins", [P, TPB, NE])
        stats = sb("stats", [P, NT, 6])
        mv = sb("mv", [P, NT, 2])
        var_eps = sb("var_eps", [P, NT])
        rstd = sb("rstd", [P, NT])
        xn = sb("xn", [P, NT, D])
        xs = sb("xs", [P, NT, 2, D], fp32r)
        xt = sb("xt", [P, 3, TOK], fp32r)
        ft_a = sb("ft_a", [P, TOK])
        ft_b = sb("ft_b", [FB + 1, TOK])
        h = sb("h", [P, NT, D])
        halves = sb("halves", [P, 2, 2 * H, 4, HS], fp32r)
        qk_t = sb("qk_t", [P, NG, 4, TOK], fp32r)
        v_aug = sb("v_aug", [P, NT, 2 * H + 1, HS])
        neg_max = sb("neg_max", [P, 2, TPB, HG])
        max_parts = sb("max_parts", [P, 2, TPB, 2, 2, SLOT], fp32r)
        probs = sb("probs", [P, 2, HG * (S + P)])
        recip = sb("recip", [P, 2, P])
        ctx_t = sb("ctx_t", [P, B, NG, P])
        best = sb("best", [P, NT])
        tie = sb("tie", [P, NT, NE])
        onehot = sb("onehot", [P, NT, NE])
        onehot_t = sb("onehot_t", [NE, TOK], fp32r)
        others_t = sb("others_t", [NE + 2, TOK], fp32r)
        hidden = sb("hidden", [P, B, HC, S])
        skip = sb("skip", [P, NT, D])
        result = sb("result", [P, NT, D])

        big = [ctx.enter_context(nc.psum_tensor(f"big{i}", [P, 3 * 512], fp32)) for i in range(2)]
        small = [ctx.enter_context(nc.psum_tensor(f"small{i}", [P, 512], fp32)) for i in range(2)]

        ORDER = [(stage, int(n)) for stage, n in (use.split() for use in (
            "tok_t 0, tok_t 1, tok 0, tok 1, split 0, x2_t 0, x2_t 1, tok_t 2, tok_t 3,"
            "qkv 0, qkv 1, low 0, tok 2, tok 3, v 0, low 1, v 1, xn 1, turn 0, turn 1, split 1,"
            "scores 0, x2_t 2, x2_t 3, qkv 2, low 2, v 2, max_t 0, scores 1, expo 0, qkv 3, low 3, v 3,"
            "max_t 1, turn 2, scores 2, turn 3, pv 0, max_t 2, expo 1, weights 0,"
            "scores 3, expo 2, pv 1, max_t 3, weights 1, scores 4, expo 3, pv 2, max_t 4, weights 2,"
            "scores 5, expo 4, proj 0, max_t 5, norm 0, pv 3, split 2, expo 5, pv 4, x3_t 0, pv 5,"
            "route 0, hidden 0, onehot_t 0, proj 1, more 0, mask 0, mask 1, more 1, mask 2,"
            "norm 1, split 3, y 0, x3_t 1, y 1, route 1, hidden 1, onehot_t 1,"
            "more 2, mask 3, mask 4, more 3, mask 5, y 2, y 3").split(","))]
        BIG_STAGES = ("qkv", "turn", "scores", "expo", "x3_t", "hidden")
        SMALL_STAGES = ("tok_t", "tok", "x2_t", "max_t", "pv", "proj", "route", "onehot_t", "y")
        BIG = [use for use in ORDER if use[0] in BIG_STAGES]

        def small_bank(use):
            if use[0] in ("tok_t", "tok", "x2_t", "y"):
                return use[1] % 2
            return int(use[0] == "pv" and use[1] not in (NG, UNITS - 1) or
                       use in (("max_t", UNITS - 1), ("route", 0), ("onehot_t", 0)))

        SMALL = [[use for use in ORDER if use[0] in SMALL_STAGES and small_bank(use) == w]
                 for w in range(2)]

        def big_use(what):
            n = BIG.index(what)
            return n % 2, n // 2

        def small_use(what):
            w = 0 if what in SMALL[0] else 1
            return w, SMALL[w].index(what)

        img_in, up_in, zero_in = sem("img_in"), sem("up_in"), sem("zero_in")
        first_in = sem("first_in")
        pad_done = sem("pad_done")
        patches_done = sem("patches_done")
        tokens_in = [sem(f"tokens_in{t}") for t in range(NT)]
        tokw_in, qkvw_in, projw_in, rw_in = sem("tokw_in"), sem("qkvw_in"), sem("projw_in"), sem("rw_in")
        projb_in, h_biased = sem("projb_in"), sem("h_biased")
        w1_in, w2_in = sem("w1_in"), sem("w2_in")
        gb_in = sem("gb_in")
        consts = sem("consts")
        idents = sem("idents")
        ones_set = sem("ones_set")
        ftb_full, ftb_done = sem("ftb_full"), sem("ftb_done")
        stats_done, aggr_done = sem("stats_done"), sem("aggr_done")
        dve_step = sem("dve_step")
        pool_step = sem("pool_step")
        var_done = sem("var_done")
        rstd_done = sem("rstd_done")
        xn_done = sem("xn_done")
        ft_done, x2t_done, x3t_done = sem("ft_done"), sem("x2t_done"), sem("x3t_done")
        hi_done, lo_done = sem("hi_done"), sem("lo_done")
        turn_full = sem("turn_full")
        turned = [sem(f"turned{g}") for g in range(NG)]
        max_split = sem("max_split")
        maxt_done = sem("maxt_done")
        slots_set = sem("slots_set")
        exp_done = sem("exp_done")
        causal_done = sem("causal_done")
        pv_out = sem("pv_out")
        qk_full = sem("qk_full")
        hidden_full = sem("hidden_full")
        v_done = sem("v_done")
        others_set, qkvw_lo_rest = sem("others_set"), sem("qkvw_lo_rest")
        qkvw_hi_done, qkvw_lo_done = sem("qkvw_hi_done"), sem("qkvw_lo_done")
        weights_hi, weights_lo = sem("weights_hi"), sem("weights_lo")
        bias_loaded, bias_split, bias_rows = sem("bias_loaded"), sem("bias_split"), sem("bias_rows")
        hid_set = sem("hid_set")
        bias_zero, bias_hi, hid_b1 = sem("bias_zero"), sem("bias_hi"), sem("hid_b1")
        xhi_done, xlo_done = sem("xhi_done"), sem("xlo_done")
        even_scores, even_shifted = sem("even_scores"), sem("even_shifted")
        onehot_done, onehott_done = sem("onehot_done"), sem("onehott_done")
        hidden_done = sem("hidden_done")
        skip_done = sem("skip_done")
        result_done = sem("result_done")
        out_done = sem("out_done")
        big_full = [sem(f"big_full{i}") for i in range(2)]
        small_full = [sem(f"small_full{i}") for i in range(2)]
        h_in, h_out, logit_in, max_done = sem("h_in"), sem("h_out"), sem("logit_in"), sem("max_done")
        warm_set, recip_done, proj_zero = sem("warm_set"), sem("recip_done"), sem("proj_zero")

        block = ctx.enter_context(nc.Block())

        def cols(t):
            return slice(P * t, P * t + P)

        def regroup(queue, t):
            i0 = B * (G // TPB) * (t % TPB) + t // TPB
            queue.dma_start(tokens[:, t, :],
                            patches[i0:i0 + B * (G // TPB) - 1:B, :, :]).then_inc(tokens_in[t], 16)

        def load_chunks(queue, dst, rows, done, blocks=1):
            for c, p0, r0, r1 in ((0, 0, 0, P), (1, 0, P, D), (1, DB, 0, DB), (2, 0, DB, D)):
                d = dst[p0:p0 + r1 - r0, c, :]
                if blocks > 1:
                    d = d.rearrange("d (e n) -> d e n", e=blocks)
                queue.dma_start(d, rows(slice(r0, r1))).then_inc(done, 16)

        @block.sync
        def _(sp):
            x_rows = x.rearrange("b c (i r) w -> b i c (r w)", r=PATCH)
            for b in range(B):
                sp.dma_start(img[b:B * G:B, :, :].rearrange("i (c r) w -> i c (r w)", c=C),
                             x_rows[b]).then_inc(img_in, 16)
            sp.dma_start(first_up[:, :, SHIFT:PATCH, :], x[:, :, 0:SHIFT, :]).then_inc(first_in, 16)
            planes = tok_w.rearrange("(q c) n -> c q n", c=F // 16)
            sp.dma_start(tokw_a[:], planes[0:P // 16]).then_inc(tokw_in, 16)
            sp.dma_start(tokw_b[0:FB, :], planes[P // 16:]).then_inc(tokw_in, 16)
            sp.wait_ge(patches_done, 4)
            for t in (0, 2):
                regroup(sp, t)
            sp.dma_start(tokw_b[FB:FB + 1, :], tok_b.rearrange("(a n) -> a n", a=1)).then_inc(tokw_in, 16)
            load_chunks(sp, qkvw, lambda r: w_attn[r], qkvw_in)
            sp.wait_ge(bias_split, 1)
            for i in range(2):
                sp.dma_start(qkv_bias[i:i + 1, :].bitcast(fp32),
                             bias_parts[:, i, 0:NB1].bitcast(fp32)).then_inc(bias_rows, 16)
                sp.dma_start(r_bias[i:i + 1, :].bitcast(fp32),
                             bias_parts[0:NE, i, NB1 + NB2:].bitcast(fp32)).then_inc(bias_rows, 16)
            sp.dma_start(projb[:], b_proj.rearrange("(a n) -> a n", a=1).to_broadcast([P, D])).then_inc(projb_in, 16)
            load_chunks(sp, rw, lambda r: router_w[r], rw_in)
            w1_v = w1.rearrange("e d n -> d e n")
            load_chunks(sp, w1_sb, lambda r: w1_v[r], w1_in, NE)
            sp.dma_start(w2_sb[:], w2.rearrange("e n d -> (e n) d").rearrange("(c p) d -> p c d", p=P))\
                .then_inc(w2_in, 16)
            sp.dma_start(b2_sb[:], b2).then_inc(w2_in, 16)
            sp.wait_ge(proj_zero, 1)
            heads = w_proj.rearrange("(g j d) n -> j d g n", g=NG, j=HG)
            for j in range(HG):
                for i in range(TPB):
                    p0 = HS * (TPB * j + i)
                    sp.dma_start(projw[p0:p0 + HS, :, i, :], heads[j]).then_inc(projw_in, 16)
            sp.wait_ge(hid_set, 1)
            for i in range(2):
                sp.dma_start(hid_rows[NE + i:NE + i + 1, :].bitcast(fp32),
                             bias_parts[:, i, NB1:NB1 + NB2].bitcast(fp32)).then_inc(hid_b1, 16)
            for t in range(NT):
                sp.wait_ge(result_done, t + 1)
                sp.dma_start(out[t // TPB, cols(t % TPB), :], result[:, t, :]).then_inc(out_done, 16)
            sp.wait_ge(out_done, 16 * NT)

        @block.gpsimd
        def _(pool):
            step = [0]

            def link(ins):
                step[0] += 1
                ins.then_inc(pool_step, 1)
                pool.wait_ge(pool_step, step[0])

            link(nc.gpsimd.memset(ident[:], 0.0))
            link(nc.gpsimd.affine_select(out=ident[:], in_=ident[:], compare_op=ALU.not_equal, fill=1.0,
                                         base=0, pattern=[[-1, P]], channel_multiplier=1))
            nc.gpsimd.tensor_copy(ident_b[:], ident[:]).then_inc(idents, 1)
            link(nc.gpsimd.memset(minus_half[:], -0.5))
            link(nc.gpsimd.memset(later[:], 0.0))
            nc.gpsimd.affine_select(out=later[:], in_=later[:], compare_op=ALU.is_ge, fill=MASKED,
                                    base=0, pattern=[[-1, P]], channel_multiplier=1).then_inc(consts, 1)
            link(nc.gpsimd.memset(ones[:], 0.0))
            nc.gpsimd.memset(ones[:, 1, :], 1.0).then_inc(consts, 1)
            nc.gpsimd.memset(bias_in[:], 0.0).then_inc(bias_zero, 1)
            pool.wait_ge(bias_zero, 1)
            with nc.allow_non_contiguous_dma(reason="small vectors"):
                pool.dma_start(bias_in[:, 0:NB1], b_attn.rearrange("(p c) -> p c", c=NB1)).then_inc(bias_loaded, 16)
                pool.dma_start(bias_in[:, NB1:NB1 + NB2],
                               b1.rearrange("e n -> (e n)").rearrange("(p c) -> p c", c=NB2)).then_inc(bias_loaded, 16)
                pool.dma_start(bias_in[0:NE, NB1 + NB2:], router_b.rearrange("(p c) -> p c", c=1))\
                    .then_inc(bias_loaded, 16)
            pool.wait_ge(patches_done, 4)
            regroup(pool, 3)
            n_rstd = [0]

            def rstds(b):
                n_rstd[0] += 1
                pool.wait_ge(var_done, n_rstd[0])
                s = slice(TPB * b, TPB * b + TPB)
                nc.gpsimd.tensor_tensor(rstd[:, s], var_eps[:, s], minus_half[:], ALU.pow).then_inc(rstd_done, 1)

            def causal(u):
                pool.wait_ge(exp_done, u + 1)
                on = probs[:, u % 2, 0:HG * S].rearrange("p (g q) -> p g q", g=HG)[:, :, 0:P]
                off = probs[:, u % 2, HG * S:].rearrange("p (g q) -> p g q", g=HG)
                for blk in (on, off):
                    nc.gpsimd.affine_select(out=blk, in_=blk, compare_op=ALU.is_ge, fill=0.0, base=0,
                                            pattern=[[0, HG], [1, P]], channel_multiplier=-1)\
                        .then_inc(causal_done, 1)

            def skips(b):
                pool.wait_ge(xn_done, 2 * NT + TPB * b + TPB)
                s = slice(TPB * b, TPB * b + TPB)
                nc.gpsimd.tensor_tensor(skip[:, s, :], h[:, s, :], xn[:, s, 0:D], ALU.add)\
                    .then_inc(skip_done, 1)

            def low_halves(lo, w, hi, c):
                return nc.gpsimd.tensor_tensor(lo[:, c, :], w[:, c, :], hi[:, c, :].bitcast(fp32), ALU.subtract)

            rstds(0)
            rstds(1)
            plain = halves[:].bitcast(fp32)
            nc.gpsimd.memset(plain[:, :, 0:H, 0, :], 0.0).then_inc(slots_set, 1)
            nc.gpsimd.memset(plain[:, :, H:2 * H, 0, 2:HS], 0.0).then_inc(slots_set, 1)
            nc.gpsimd.memset(plain[:, :, H:2 * H, 0, 0:2], 1.0).then_inc(slots_set, 1)
            for stage, n in ORDER:
                if stage == "expo":
                    causal(n)
                if stage == "tok" and n % TPB == TPB - 1:
                    rstds(n // TPB)
                    if n > TPB:
                        nc.gpsimd.memset(projw[:], 0.0).then_inc(proj_zero, 1)
                    if n < TPB:
                        pool.wait_ge(qkvw_hi_done, 1)
                        low_halves(qkvw_lo, qkvw, qkvw_hi, 0).then_inc(qkvw_lo_done, 1)
                if stage == "qkv" and n == 0:
                    nc.gpsimd.memset(max_parts[:].bitcast(fp32), 0.0).then_inc(consts, 1)
                    link(nc.gpsimd.memset(expert_rows[:], 0.0))
                    ev = expert_rows[:].rearrange("e (f n) -> e f n", f=NE)
                    nc.gpsimd.affine_select(out=ev, in_=ev, compare_op=ALU.not_equal, fill=OFF, base=0,
                                            pattern=[[-1, NE], [0, HID]], channel_multiplier=1).then_inc(consts, 1)
                    for e in range(NE):
                        link(nc.gpsimd.memset(first_wins[:, :, e:e + 1], float(NE - e)))
                if (stage, n) == ("scores", 0):
                    pool.wait_ge(projb_in, 16)
                    for b in range(B):
                        pool.wait_ge(xn_done, NT + TPB * b + TPB)
                        s = slice(TPB * b, TPB * b + TPB)
                        nc.gpsimd.tensor_tensor(h[:, s, :], h[:, s, :], projb[:].unsqueeze(1).to_broadcast([P, TPB, D]),
                                                ALU.add).then_inc(h_biased, 1)
                if (stage, n) == ("weights", 0):
                    pool.wait_ge(weights_hi, 2)
                    for c in range(2):
                        low_halves(rw_lo, rw, rw_hi, c).then_inc(weights_lo, 1)
                    nc.gpsimd.tensor_tensor(b2_lo[:], b2_sb[:], b2_hi[:].bitcast(fp32), ALU.subtract)\
                        .then_inc(weights_lo, 1)
                if stage == "weights" and n < 2:
                    pool.wait_ge(weights_hi, 3 + n)
                    low_halves(w1_lo, w1_sb, w1_hi, n).then_inc(weights_lo, 1)
                if stage == "proj":
                    rstds(n)
                    skips(n)

        @block.scalar
        def _(act):
            def affine_in(n, vec):
                planes = vec.rearrange("(q c a) -> c q a", c=F // 16, a=1)
                with nc.allow_non_contiguous_dma(reason="a small vector"):
                    act.dma_start(gb_a[:, n:n + 1], planes[0:P // 16]).then_inc(gb_in, 16)
                    act.dma_start(gb_b[0:FB, n:n + 1], planes[P // 16:]).then_inc(gb_in, 16)

            for b in range(B):
                rows = x[b, :, SHIFT:IMG - SHIFT, :].rearrange("c (i r) w -> i c (r w)", r=PATCH)
                act.dma_start(img_up[B + b:B * G:B, :, :].rearrange("i (c r) w -> i c (r w)", c=C),
                              rows).then_inc(up_in, 16)
            affine_in(0, tok_gamma)
            act.wait_ge(patches_done, 4)
            regroup(act, 1)
            affine_in(1, tok_beta)
            act.wait_ge(warm_set, 1)
            nc.scalar.activation(first_act[:], warm[:, 0:1], ACT.Identity)

            def small_in(what):
                w, n = small_use(what)
                act.wait_ge(small_full[w], n + 1)
                return w

            def tok_turned(t):
                w = small_in(("tok_t", t))
                nc.scalar.activation(ft_a[:, cols(t)], small[w][:, 0:P], ACT.Identity, bias=gb_a[:, 1:2],
                                     scale=gb_a[:, 0:1]).then_inc(ft_done, 1)

            def turned_copy(t):
                w = small_in(("x2_t", t))
                nc.scalar.activation(xt[:, :, cols(t)], small[w][:, 0:3 * P].rearrange("p (c q) -> p c q", c=3),
                                     ACT.Copy).then_inc(x2t_done, 1)

            def x_high(n):
                for t in range(TPB * (n % B), TPB * (n % B) + TPB):
                    act.wait_ge(xn_done, NT * (1 + n // B) + t + 1)
                    nc.scalar.activation(xs[:, t, 0, :], xn[:, t, :], ACT.Copy).then_inc(xhi_done, 1)

            def split_high(t):
                a, n = big_use(("qkv", t))
                act.wait_ge(qk_full, t + 1)
                if t >= 2:
                    a2, n2 = big_use(("turn", t - 2))
                    act.wait_ge(big_full[a2], n2 + 1)
                q = big[a][:, 0:D].rearrange("p (n d) -> p n d", n=H)
                k = big[a][:, D:2 * D].rearrange("p (n d) -> p n d", n=H)
                nc.scalar.activation(halves[:, t % 2, 0:H, 1:3, :], q.unsqueeze(2).to_broadcast([P, H, 2, HS]),
                                     ACT.Copy).then_inc(hi_done, 1)
                nc.scalar.activation(halves[:, t % 2, H:2 * H, 1:4:2, :],
                                     k.unsqueeze(2).to_broadcast([P, H, 2, HS]), ACT.Copy).then_inc(hi_done, 1)

            def values_in(t):
                a, n = big_use(("qkv", t))
                act.wait_ge(big_full[a], n + 1)
                v = big[a][:, 512:512 + D].rearrange("p (n d) -> p n d", n=H)
                nc.scalar.activation(v_aug[:, t, 1:2 * H:2, :], v, ACT.Copy).then_inc(v_done, 1)

            def turned_halves(t):
                a, m = big_use(("turn", t))
                for g in (0, 2):
                    if g == 0:
                        act.wait_ge(turn_full, 2 * t + 1)
                    else:
                        act.wait_ge(big_full[a], m + 1)
                    nc.scalar.activation(qk_t[:, g, :, cols(t)],
                                         big[a][:, 512 * g:512 * g + 512].rearrange("p (n q) -> p n q", n=4),
                                         ACT.Copy).then_inc(turned[g], 1)

            def max_rows(u):
                w = small_in(("max_t", u))
                b, g = u // NG, u % NG
                for r0 in (0, SLOT):
                    nc.scalar.activation(qk_t[r0:r0 + 2, g, 0:2, S * b:S * b + S],
                                         small[w][r0:r0 + 2, :].rearrange("p (n q) -> p n q", n=2),
                                         ACT.Copy).then_inc(maxt_done, 1)

            def exps(u):
                a, n = big_use(("expo", u))
                act.wait_ge(big_full[a], n + 1)
                if u >= 2:
                    w, m = small_use(("pv", u - 2))
                    act.wait_ge(small_full[w], m + 1)
                nc.scalar.activation(probs[:, u % 2, :], big[a][:, :], ACT.Exp, scale=SCALE).then_inc(exp_done, 1)

            def gelu(n):
                b, c = n // (HC // 2), n % (HC // 2) * 2
                a, _ = big_use(("hidden", b))
                act.wait_ge(hidden_full, n + 1)
                nc.scalar.activation(hidden[:, b, c:c + 2, :],
                                     big[a][:, S * c:S * (c + 2)].rearrange("p (c q) -> p c q", c=2),
                                     ACT.Gelu).then_inc(hidden_done, 1)

            def qkvw_high(c):
                nc.scalar.activation(qkvw_hi[:, c, :], qkvw[:, c, :], ACT.Copy).then_inc(qkvw_hi_done, 1)

            act.wait_ge(gb_in, 16 * 4)
            act.wait_ge(ones_set, 2)
            for stage, n in ORDER:
                if stage == "tok_t":
                    tok_turned(n)
                if (stage, n) == ("tok_t", 1):
                    act.wait_ge(qkvw_in, 16 * 4)
                    qkvw_high(0)
                    qkvw_high(1)
                if stage == "weights":
                    if n == 0:
                        act.wait_ge(rw_in, 16 * 4)
                        nc.scalar.activation(rw_hi[:], rw[:], ACT.Copy).then_inc(weights_hi, 1)
                        act.wait_ge(w2_in, 16 * 2)
                        nc.scalar.activation(b2_hi[:], b2_sb[:], ACT.Copy).then_inc(weights_hi, 1)
                        act.wait_ge(w1_in, 16 * 4)
                    nc.scalar.activation(w1_hi[:, n, :], w1_sb[:, n, :], ACT.Copy).then_inc(weights_hi, 1)
                if stage == "split":
                    x_high(n)
                if (stage, n) == ("split", 0):
                    qkvw_high(2)
                if stage == "tok" and n >= TPB:
                    w = small_in(("tok", n))
                    act.wait_ge(stats_done, NT + n + 1)
                    nc.scalar.activation(h[:, n, :], small[w][:, 0:D], ACT.Copy).then_inc(h_in, 1)
                if stage == "x2_t":
                    turned_copy(n)
                if stage == "qkv":
                    split_high(n)
                if stage == "v":
                    values_in(n)
                if stage == "turn":
                    turned_halves(n)
                if stage == "max_t":
                    max_rows(n)
                if stage == "expo":
                    exps(n)
                if stage == "x3_t":
                    a, m = big_use(("x3_t", n))
                    act.wait_ge(big_full[a], m + 1)
                    for i in range(TPB):
                        nc.scalar.activation(xt[:, :, cols(TPB * n + i)],
                                             big[a][:, 512 * i:512 * i + 3 * P].rearrange("p (c q) -> p c q", c=3),
                                             ACT.Copy).then_inc(x3t_done, 1)
                if stage == "mask":
                    gelu(n)

        @block.vector
        def _(dve):
            step = [0]

            def link(ins):
                step[0] += 1
                ins.then_inc(dve_step, 1)
                dve.wait_ge(dve_step, step[0])

            def small_in(what):
                w, n = small_use(what)
                dve.wait_ge(small_full[w], n + 1)
                return w

            def big_in(what):
                a, n = big_use(what)
                dve.wait_ge(big_full[a], n + 1)
                return a

            nc.vector.memset(warm[:], 0.0).then_inc(warm_set, 1)
            nc.vector.memset(first_up[:, :, 0:SHIFT, :], 0.0).then_inc(zero_in, 1)
            nc.vector.memset(patches[:, 0, 2 * FK:3 * FK], 0.0).then_inc(pad_done, 1)
            nc.vector.memset(ft_b[:], 1.0).then_inc(ones_set, 1)
            dve.wait_ge(idents, 1)
            nc.vector.tensor_copy(ident_r[:], ident[:]).then_inc(idents, 1)

            def patch_view(k, j0=0):
                return patches[:, j0:G, FK * k:FK * k + FK].rearrange("p j (r c) -> p j r c", c=PATCH)

            dve.wait_ge(img_in, 16 * B)
            nc.vector.tensor_copy(patch_view(0), img[:].rearrange("p r (j c) -> p j r c", c=PATCH))\
                .then_inc(patches_done, 1)
            nc.vector.tensor_copy(
                patch_view(2, 1),
                img[:, :, SHIFT:IMG - SHIFT].rearrange("p r (j c) -> p j r c", c=PATCH)).then_inc(patches_done, 1)
            dve.wait_ge(pad_done, 1)
            nc.vector.tensor_copy(patch_view(2)[:, 0, :, SHIFT:PATCH], img[:, :, 0:SHIFT]).then_inc(patches_done, 1)
            dve.wait_ge(up_in, 16 * B)
            dve.wait_ge(first_in, 16)
            dve.wait_ge(zero_in, 1)
            nc.vector.tensor_copy(patch_view(1), img_up[:].rearrange("p r (j c) -> p j r c", c=PATCH))\
                .then_inc(patches_done, 1)

            n_rstd = [0]
            stats_of = [0]

            def variances(b, eps):
                ts = range(TPB * b, TPB * b + TPB)
                stats_of[0] += TPB
                dve.wait_ge(stats_done, stats_of[0])
                for t in ts:
                    nc.vector.bn_aggr(mv[:, t, :], stats[:, t, :]).then_inc(aggr_done, 1)
                dve.wait_ge(aggr_done, stats_of[0])
                nc.vector.tensor_scalar(var_eps[:, ts[0]:ts[-1] + 1], mv[:, ts[0]:ts[-1] + 1, 1], eps, None,
                                        ALU.add).then_inc(var_done, 1)

            def normalise(src, b, width):
                n_rstd[0] += 1
                dve.wait_ge(rstd_done, n_rstd[0])
                for t in range(TPB * b, TPB * b + TPB):
                    nc.vector.tensor_scalar(xn[:, t, 0:width], src[:, t, :], mv[:, t, 0:1], rstd[:, t:t + 1],
                                            ALU.subtract, ALU.mult).then_inc(xn_done, 1)

            def split_low(t):
                a, _ = big_use(("qkv", t))
                dve.wait_ge(hi_done, 2 * t + 2)
                q = big[a][:, 0:D].rearrange("p (n d) -> p n d", n=H)
                k = big[a][:, D:2 * D].rearrange("p (n d) -> p n d", n=H)
                for x_, rows, hi, lo in ((q, slice(0, H), 1, 3), (k, slice(H, 2 * H), 1, 2)):
                    nc.vector.tensor_tensor(halves[:, t % 2, rows, lo, :], x_, halves[:, t % 2, rows, hi, :].bitcast(fp32),
                                            ALU.subtract).then_inc(lo_done, 1)

            def turned_halves(t):
                a, _ = big_use(("turn", t))
                dve.wait_ge(turn_full, 2 * t + 2)
                nc.vector.tensor_copy(qk_t[:, 1, :, cols(t)],
                                      big[a][:, 512:2 * 512].rearrange("p (n q) -> p n q", n=4)).then_inc(turned[1], 1)

            def maxima(u):
                a = big_in(("scores", u))
                if u >= 2:
                    w, n = small_use(("max_t", u - 2))
                    dve.wait_ge(small_full[w], n + 1)
                p = u % 2
                nc.vector.tensor_reduce(neg_max[:, p, 0, :],
                                        big[a][:, 2 * 512:3 * 512].rearrange("p (g k) -> p g k", g=HG),
                                        AX.X, ALU.max, negate=True).then_inc(max_done, 1)
                nc.vector.tensor_reduce(neg_max[:, p, 1, :],
                                        big[a][:, 0:2 * 512].rearrange("p (g k) -> p g k", g=HG),
                                        AX.X, ALU.max, negate=True).then_inc(max_done, 1)
                dve.wait_ge(max_done, 2 * u + 2)
                whole = neg_max[:, p, :, :].rearrange("p i (o n) -> p i o n", o=2)
                high, low = (max_parts[:, p, :, :, :, c].rearrange("p i n o -> p i o n") for c in range(2))
                link(nc.vector.tensor_copy(high, whole))
                nc.vector.tensor_tensor(low, whole, high.bitcast(fp32), ALU.subtract).then_inc(max_split, 1)

            def context(u):
                w = small_in(("pv", u))
                nc.vector.reciprocal(recip[:, u % 2, :], small[w][:, P:2 * P]).then_inc(recip_done, 1)
                dve.wait_ge(recip_done, u + 1)
                nc.vector.tensor_tensor(ctx_t[:, u // NG, u % NG, :], small[w][:, 0:P], recip[:, u % 2, :],
                                        ALU.mult).then_inc(pv_out, 1)

            def attention_out(b):
                w = small_in(("proj", b))
                dve.wait_ge(h_biased, b + 1)
                s = slice(TPB * b, TPB * b + TPB)
                nc.vector.tensor_tensor(h[:, s, :], small[w][:, 0:TPB * D].rearrange("p (t d) -> p t d", t=TPB),
                                        h[:, s, :], ALU.add).then_inc(h_out, 1)
                dve.wait_ge(h_out, b + 1)
                for t in (TPB * b, TPB * b + 1):
                    nc.vector.bn_stats(stats[:, t, :], h[:, t, :]).then_inc(stats_done, 1)

            def route(b):
                w = small_in(("route", b))
                s = slice(TPB * b, TPB * b + TPB)
                logit = small[w][:, 0:TPB * NE].rearrange("p (t e) -> p t e", t=TPB)
                top = best[:, s].unsqueeze(2).to_broadcast([P, TPB, NE])
                link(nc.vector.tensor_reduce(best[:, s], logit, AX.X, ALU.max))
                nc.vector.tensor_tensor(tie[:, s, :], logit, top, ALU.is_equal).then_inc(logit_in, 1)
                dve.wait_ge(logit_in, b + 1)
                link(nc.vector.tensor_tensor(tie[:, s, :], tie[:, s, :], first_wins[:], ALU.mult))
                link(nc.vector.tensor_reduce(best[:, s], tie[:, s, :], AX.X, ALU.max))
                nc.vector.tensor_tensor(onehot[:, s, :], tie[:, s, :], top, ALU.is_equal)\
                    .then_inc(onehot_done, 1)

            def onehot_rows(b):
                w = small_in(("onehot_t", b))
                s = slice(S * b, S * b + S)
                dve.wait_ge(others_set, 1)
                nc.vector.tensor_scalar(others_t[0:NE, s], small[w][0:NE, 0:S], 1.0, None,
                                        ALU.subtract).then_inc(onehott_done, 1)
                nc.vector.tensor_copy(onehot_t[:, s], small[w][0:NE, 0:S]).then_inc(onehott_done, 1)

            def last_sum(t):
                w = small_in(("y", t))
                dve.wait_ge(skip_done, t // TPB + 1)
                nc.vector.tensor_tensor(result[:, t, :], small[w][:, 0:D], skip[:, t, :],
                                        ALU.add).then_inc(result_done, 1)

            nc.vector.memset(v_aug[:, :, 0:2 * H + 1:2, :], 0.0).then_inc(ones_set, 1)
            dve.wait_ge(bias_loaded, 16 * 3)
            nc.vector.tensor_copy(bias_parts[:, 0, :], bias_in[:]).then_inc(bias_hi, 1)
            dve.wait_ge(bias_hi, 1)
            nc.vector.tensor_tensor(bias_parts[:, 1, :], bias_in[:], bias_parts[:, 0, :].bitcast(fp32),
                                    ALU.subtract).then_inc(bias_split, 1)
            nc.vector.memset(ones_r[:].bitcast(fp32), 1.0).then_inc(ones_set, 1)

            def tok_turned(t):
                dve.wait_ge(gb_in, 16 * 4)
                dve.wait_ge(ones_set, 1)
                dve.wait_ge(ftb_full, t + 1)
                nc.vector.tensor_scalar(ft_b[0:FB, cols(t)], big[1][0:FB, 512 * (t % 2):512 * (t % 2) + P],
                                        gb_b[:, 0:1], gb_b[:, 1:2], ALU.mult, ALU.add).then_inc(ftb_done, 1)

            for b in range(B):
                for t in (TPB * b, TPB * b + 1):
                    dve.wait_ge(tokens_in[t], 16)
                    nc.vector.bn_stats(stats[:, t, :], tokens[:, t, :]).then_inc(stats_done, 1)
                variances(b, TOK_EPS)
                if b == 0:
                    normalise(tokens, b, F)
            for stage, n in ORDER:
                if stage == "tok":
                    w = small_in(("tok", n))
                    nc.vector.bn_stats(stats[:, n, :], small[w][:, 0:D]).then_inc(stats_done, 1)
                if stage == "proj":
                    attention_out(n)
                if stage == "tok" and n % TPB == TPB - 1:
                    variances(n // TPB, EPS)
                    if n < TPB:
                        for t in (n - 1, n):
                            w, _ = small_use(("tok", t))
                            nc.vector.tensor_copy(h[:, t, :], small[w][:, 0:D]).then_inc(h_in, 1)
                        dve.wait_ge(h_in, n + 1)
                        normalise(h, 0, D)
                if stage == "xn":
                    dve.wait_ge(h_in, TPB * (n + 1))
                    normalise(h, n, D)
                if stage == "proj":
                    variances(n, EPS)
                if stage == "tok_t":
                    tok_turned(n)
                if (stage, n) == ("tok_t", 1):
                    normalise(tokens, 1, F)
                if stage == "norm":
                    normalise(h, n, D)
                if stage == "split":
                    for t in range(TPB * (n % B), TPB * (n % B) + TPB):
                        dve.wait_ge(xhi_done, NT * (n // B) + t + 1)
                        nc.vector.tensor_tensor(xs[:, t, 1, :], xn[:, t, :], xs[:, t, 0, :].bitcast(fp32),
                                                ALU.subtract).then_inc(xlo_done, 1)
                    if n == 0:
                        dve.wait_ge(qkvw_hi_done, 2)
                        nc.vector.tensor_tensor(qkvw_lo[:, 1, :], qkvw[:, 1, :], qkvw_hi[:, 1, :].bitcast(fp32),
                                                ALU.subtract).then_inc(qkvw_lo_rest, 1)
                if (stage, n) == ("expo", UNITS - 1):
                    nc.vector.memset(others_t[:].bitcast(fp32), 1.0).then_inc(others_set, 1)
                    dve.wait_ge(consts, 4)
                    nc.vector.tensor_copy(hid_rows[:], expert_rows[:]).then_inc(hid_set, 1)
                if stage == "low":
                    split_low(n)
                if stage == "turn":
                    turned_halves(n)
                if stage == "scores":
                    if n == 0:
                        dve.wait_ge(consts, 4)
                    maxima(n)
                if stage == "pv":
                    context(n)
                if stage == "route":
                    route(n)
                if stage == "onehot_t":
                    onehot_rows(n)
                if stage == "y":
                    last_sum(n)

        @block.tensor
        def _(pe):
            def read_by(what):
                stage, n = what
                return {
                    "tok_t": (ft_done, n + 1), "tok": (h_in, n + 1), "x2_t": (x2t_done, n + 1),
                    "qkv": (lo_done, 2 * n + 2), "turn": (turned[0], n + 1),
                    "scores": (max_done, 2 * n + 2), "max_t": (maxt_done, 2 * n + 2),
                    "expo": (exp_done, n + 1), "pv": (pv_out, n + 1),
                    "proj": (h_out, n + 1),
                    "x3_t": (x3t_done, 2 * n + 2), "route": (logit_in, n + 1),
                    "onehot_t": (onehott_done, 2 * n + 2), "hidden": (hidden_done, HC // 2 * (n + 1)),
                    "y": (result_done, n + 1),
                }[stage]

            def ready(what):
                w, n = small_use(what)
                if n:
                    pe.wait_ge(*read_by(SMALL[w][n - 1]))
                return w

            def big_ready(what):
                a, n = big_use(what)
                if n:
                    last = BIG[2 * (n - 1) + a]
                    pe.wait_ge(*read_by(last))
                    if last[0] == "qkv":
                        pe.wait_ge(v_done, last[1] + 1)
                    if last[0] == "turn":
                        pe.wait_ge(turned[1], last[1] + 1)
                        pe.wait_ge(turned[2], last[1] + 1)
                return a

            def mm(o, l, r, start=True, stop=True, **k):
                return nc.tensor.matmul(o, l, r, start=start, stop=stop, **k)

            def turn_tokens(t):
                w = ready(("tok_t", t))
                nc.tensor.transpose(small[w][:, 0:P], xn[:, t, 0:P], ident[:]).then_inc(small_full[w], 1)
                if t >= 2:
                    pe.wait_ge(ftb_done, t - 1)
                nc.tensor.transpose(big[1][0:FB, 512 * (t % 2):512 * (t % 2) + P], xn[:, t, P:F], ident[:])\
                    .then_inc(ftb_full, 1)

            def turn_rows(o, t):
                rows = xs[:, t, :, :].rearrange("p s d -> p (s d)")
                for c in range(3):
                    last = nc.tensor.transpose(o[:, P * c:P * c + P].bitcast(fp32r), rows[:, P * c:P * c + P],
                                               ident_r[:])
                return last

            def products(c0, c1, w_hi, w_lo):
                return [(k, w[:, k, c0:c1]) for k, w in ((0, w_hi), (1, w_hi), (2, w_hi), (0, w_lo), (1, w_lo))]

            def rows_out(what, xa, xb, wa, wb, width):
                w = ready(what)
                t = what[1]
                mm(small[w][:, 0:width], xa[:, cols(t)], wa, stop=False)
                mm(small[w][:, 0:width], xb[:, cols(t)], wb, start=False).then_inc(small_full[w], 1)

            def qkv(t, o, c0, c1):
                a, _ = big_use(("qkv", t))
                mm(big[a][:, o:o + c1 - c0], ones_r[:], qkv_bias[:, c0:c1], stop=False)
                for n, (k, w) in enumerate(products(c0, c1, qkvw_hi, qkvw_lo)):
                    if t == 0 and n == 3:
                        pe.wait_ge(qkvw_lo_done, 1)
                        pe.wait_ge(qkvw_lo_rest, 1)
                    last = mm(big[a][:, o:o + c1 - c0], xt[:, k, cols(t)], w, start=False, stop=(n == 4))
                return last

            def turn_halves(t):
                a = big_ready(("turn", t))
                pe.wait_ge(lo_done, 2 * t + 2)
                pe.wait_ge(hi_done, 2 * t + 2)
                pe.wait_ge(slots_set, 3)
                for g in range(NG):
                    for i in range(4):
                        n = PAIRS * (i // 2) + 2 * g + i % 2
                        last = nc.tensor.transpose(
                            big[a][:, 512 * g + P * i:512 * g + P * i + P].bitcast(fp32r),
                            halves[:, t % 2, 2 * n:2 * n + 2, :, :].rearrange("p n s d -> p (n s d)"), ident_r[:])
                    if g < NG - 1:
                        last.then_inc(turn_full, 1)
                last.then_inc(big_full[a], 1)

            def qk(hd, which, b, c0, c1):
                r = SLOT * (hd % 2)
                return qk_t[r:r + SLOT, hd // HG, 2 * which + hd % HG // 2, S * b + c0:S * b + c1]

            def scores(u):
                a = big_ready(("scores", u))
                b, g = u // NG, u % NG
                areas = [(big[a][:, 0:512].rearrange("p (g k) -> p g k", g=2), S, P),
                         (big[a][:, 512:1024].rearrange("p (g k) -> p g k", g=2), S, P),
                         (big[a][:, 1024:1536].rearrange("p (g k) -> p g k", g=HG), P, 0)]
                for area, width, q0 in areas:
                    mm(area[:, :, width - P:width], ident_b[:],
                       later[:].unsqueeze(1).to_broadcast([P, 512 // width, P]), skip_group_check=True)
                pe.wait_ge(turned[g], TPB * (b + 1))
                for n, odd, j in ((2, 0, 0), (2, 0, 1), (1, 1, 0), (0, 0, 0), (1, 1, 1), (0, 0, 1), (2, 1, 0), (2, 1, 1)):
                    area, width, q0 = areas[n]
                    if (n, odd, j) == (2, 1, 0):
                        pe.wait_ge(even_scores, u + 1)
                    hd = HG * g + 2 * j + odd
                    last = mm(area[:, (2 * odd if n == 2 else 0) + j, :], qk(hd, 0, b, q0, q0 + P),
                              qk(hd, 1, b, 0, width), start=False, skip_group_check=True)
                    if (n, odd, j) == (2, 0, 1):
                        last.then_inc(even_scores, 1)
                last.then_inc(big_full[a], 1)

            def max_rows(u):
                w = ready(("max_t", u))
                pe.wait_ge(max_split, u + 1)
                for i in range(TPB):
                    for n in range(2):
                        c = S * n + P * i
                        last = nc.tensor.transpose(
                            small[w][0:SLOT + 2, c:c + P].bitcast(fp32r),
                            max_parts[:, u % 2, i, n, :, :].rearrange("p o s -> p (o s)")[:, 0:SLOT + 2], ident_r[:])
                last.then_inc(small_full[w], 1)

            def shifted_scores(u):
                a = big_ready(("expo", u))
                b, g = u // NG, u % NG
                pe.wait_ge(maxt_done, 2 * u + 2)

                def place(j, k0):
                    c = (512 * (j % 2) + S * (j // 2)) if k0 == 0 else 1024 + P * (2 * (j % 2) + j // 2)
                    return big[a][:, c:c + S - k0]

                for k0, j in ((P, 0), (P, 2), (0, 1), (0, 0), (0, 3), (0, 2), (P, 1), (P, 3)):
                    if (k0, j) == (P, 1):
                        pe.wait_ge(even_shifted, u + 1)
                    hd = HG * g + j
                    last = mm(place(j, k0), qk(hd, 1, b, k0, k0 + P), qk(hd, 0, b, k0, S),
                              skip_group_check=True)
                    if (k0, j) == (P, 2):
                        last.then_inc(even_shifted, 1)
                last.then_inc(big_full[a], 1)

            def values(u):
                w = ready(("pv", u))
                b, g = u // NG, u % NG
                for of_ones in (0, 1):
                    for k, i in ((0, 0), (0, 1), (1, 1)):
                        if not of_ones:
                            pe.wait_ge(causal_done, 2 * u + k + 1)
                        for j in range(HG):
                            n = 2 * (j % 2) + j // 2
                            c = S * n + P * i if k == 0 else HG * S + P * n
                            v = ones[:, 1 - i:3 - i, :] if of_ones else \
                                v_aug[:, TPB * b + k, 2 * (HG * g + j) + 1 - i:2 * (HG * g + j) + 3 - i, :]
                            last = mm(small[w][32 * j:32 * j + 32, P * of_ones:P * of_ones + P],
                                      v.rearrange("p s d -> p (s d)"), probs[:, u % 2, c:c + P],
                                      start=(i == 0), stop=(k == 1), skip_group_check=True)
                last.then_inc(small_full[w], 1)

            def project(b):
                w = ready(("proj", b))
                pe.wait_ge(pv_out, NG * (b + 1))
                for g in range(NG):
                    last = mm(small[w][:, 0:TPB * D], ctx_t[:, b, g, :],
                              projw[:, g, :, :].rearrange("p i n -> p (i n)"), start=(g == 0), stop=(g == NG - 1))
                last.then_inc(small_full[w], 1)

            def hidden_in(b, chunks):
                a, _ = big_use(("hidden", b))
                s = slice(S * b, S * b + S)
                for c in chunks:
                    o = big[a][:, S * c:S * c + S]
                    for n, (k, w) in enumerate(products(P * c, P * c + P, w1_hi, w1_lo)):
                        mm(o, w, xt[:, k, s], start=(c % 2 == 0 and n == 0), skip_group_check=True)

            def mask_experts(n):
                b, c0 = n // (HC // 2), n % (HC // 2) * 2
                a, _ = big_use(("hidden", b))
                pe.wait_ge(onehott_done, 2 * b + 1)
                s = slice(S * b, S * b + S)
                for c in (c0, c0 + 1):
                    last = mm(big[a][:, S * c:S * c + S], hid_rows[:, P * c:P * c + P], others_t[:, s],
                              start=False, skip_group_check=True)
                last.then_inc(hidden_full, 1)

            def experts_out(t):
                w = ready(("y", t))
                b = t // TPB
                pe.wait_ge(onehott_done, 2 * b + 2)
                mm(small[w][:, 0:D], onehot_t[:, cols(t)], b2_hi[:], stop=False)
                mm(small[w][:, 0:D], onehot_t[:, cols(t)], b2_lo[:], start=False, stop=False)
                for c in range(HC):
                    if c % 2 == 0:
                        pe.wait_ge(hidden_done, (HC * b + c) // 2 + 1)
                    last = mm(small[w][:, 0:D], hidden[:, b, c, cols(t % TPB)], w2_sb[:, c, :],
                              start=False, stop=(c == HC - 1))
                last.then_inc(small_full[w], 1)

            def keep_warm(n):
                for i in range(n):
                    mm(big[1][:, 1024:1536], warm[:, 0:P], warm[:])

            pe.wait_ge(warm_set, 1)
            keep_warm(START)
            pe.wait_ge(idents, 2)
            pe.wait_ge(ones_set, 2)
            for stage, n in ORDER:
                if (stage, n) in STEADY:
                    use, count = STEADY[stage, n]
                    w = ready(use)
                    for i in range(count):
                        mm(small[w][:, :], warm[:, 0:P], warm[:])
                if stage == "tok_t":
                    pe.wait_ge(xn_done, n + 1)
                    turn_tokens(n)
                if stage == "tok":
                    pe.wait_ge(tokw_in, 16 * 3)
                    pe.wait_ge(ft_done, n + 1)
                    pe.wait_ge(ftb_done, n + 1)
                    rows_out(("tok", n), ft_a, ft_b, tokw_a[:], tokw_b[:], D)
                if stage == "x2_t":
                    w = ready(("x2_t", n))
                    pe.wait_ge(xlo_done, n + 1)
                    turn_rows(small[w], n).then_inc(small_full[w], 1)
                if stage == "qkv":
                    pe.wait_ge(qkvw_hi_done, 3)
                    pe.wait_ge(bias_rows, 16 * 4)
                    big_ready(("qkv", n))
                    if n == 1:
                        pe.wait_ge(ftb_done, NT)
                    keep_warm(BEFORE.get((stage, n), 0))
                    pe.wait_ge(x2t_done, n + 1)
                    qkv(n, 0, 0, 2 * D).then_inc(qk_full, 1)
                if stage == "v":
                    a, _ = big_use(("qkv", n))
                    qkv(n, 512, 2 * D, 3 * D).then_inc(big_full[a], 1)
                if stage == "turn":
                    turn_halves(n)
                if stage == "scores":
                    pe.wait_ge(consts, 4)
                    pe.wait_ge(ones_set, 3)
                    scores(n)
                if stage == "max_t":
                    max_rows(n)
                if stage == "expo":
                    shifted_scores(n)
                if stage == "pv":
                    values(n)
                if stage == "proj":
                    pe.wait_ge(projw_in, 16 * TPB * HG)
                    project(n)
                if stage == "x3_t":
                    a = big_ready(("x3_t", n))
                    pe.wait_ge(xlo_done, NT + TPB * (n + 1))
                    turn_rows(big[a], TPB * n)
                    turn_rows(big[a][:, 512:], TPB * n + 1).then_inc(big_full[a], 1)
                if stage == "route":
                    w = ready(("route", n))
                    pe.wait_ge(weights_lo, 2)
                    pe.wait_ge(x3t_done, 2 * n + 2)
                    for i in range(TPB):
                        o = small[w][:, NE * i:NE * i + NE]
                        mm(o, ones_r[:], r_bias[:], stop=False)
                        for j, (k, rws) in enumerate(products(0, NE, rw_hi, rw_lo)):
                            last = mm(o, xt[:, k, cols(TPB * n + i)], rws, start=False, stop=(j == 4))
                    last.then_inc(small_full[w], 1)
                if stage == "onehot_t":
                    w = ready(("onehot_t", n))
                    pe.wait_ge(onehot_done, n + 1)
                    for i in range(TPB):
                        last = nc.tensor.transpose(small[w][0:NE, P * i:P * i + P], onehot[:, TPB * n + i, :],
                                                   ident[:])
                    last.then_inc(small_full[w], 1)
                if stage == "hidden":
                    pe.wait_ge(weights_hi, 5)
                    pe.wait_ge(weights_lo, 5)
                    big_ready(("hidden", n))
                    pe.wait_ge(x3t_done, 2 * n + 2)
                    hidden_in(n, (0, 1))
                if stage == "more":
                    c = 2 + 2 * (n % 2)
                    hidden_in(n // 2, (c, c + 1))
                if stage == "mask":
                    pe.wait_ge(hid_b1, 16 * 2)
                    mask_experts(n)
                if stage == "y":
                    pe.wait_ge(w2_in, 16 * 2)
                    pe.wait_ge(weights_lo, 5)
                    experts_out(n)
                keep_warm(FILL.get((stage, n), 0))


_INS = ['x', 'L0_tok_ln_gamma', 'L0_tok_ln_beta', 'L0_tok_W', 'L0_tok_b', 'L0_attn_W_attn', 'L0_attn_b_attn',
        'L0_attn_W_proj', 'L0_attn_b_proj', 'L0_ffn_router_w', 'L0_ffn_router_b', 'L0_ffn_w1', 'L0_ffn_b1',
        'L0_ffn_w2', 'L0_ffn_b2']


def kernel(**inputs):
    import numpy as _np
    import concourse.bacc as _bacc
    from concourse import mybir as _mybir
    from concourse.bass_utils import run_bass_kernel_spmd as _run

    nc = _bacc.Bacc("TRN2", target_bir_lowering=False, num_devices=1)
    arrays, args = {}, []
    for name in _INS:
        a = _np.ascontiguousarray(inputs[name])
        arrays[f"in_{name}_dram"] = a
        args.append(nc.dram_tensor(f"in_{name}_dram", a.shape, _mybir.dt.from_np(a.dtype), kind="ExternalInput").ap())
    out = nc.dram_tensor("out_dram", (2, 256, 192), _mybir.dt.float32, kind="ExternalOutput").ap()
    vit_tower(nc, *args, out)
    r = _run(nc, [arrays], core_ids=[0])
    return r.results[0]["out_dram"]
```
